# Optimizing a Trainium2 kernel written in Bass

```python
import numpy as np
import jax
import jax.numpy as jnp

def _softmax(x, axis=-1):
    return jax.nn.softmax(x, axis=axis)

def _gelu(x):
    return jax.nn.gelu(x, approximate=True)

def _silu(x):
    return jax.nn.silu(x)

def _sigmoid(x):
    return jax.nn.sigmoid(x)

def _layernorm(x, axis=-1, eps=1e-05):
    m = jnp.mean(x, axis=axis, keepdims=True)
    v = jnp.var(x, axis=axis, keepdims=True)
    return (x - m) / jnp.sqrt(v + eps)

def _scatter_add(tgt, idx, src, axis=0):
    return tgt.at[idx].add(src)

def _segment_sum(src, seg, n):
    return jax.ops.segment_sum(src, seg, n)
kernel_name = 'mk_macaron_d1_jaxref_r8_d1b569'

def setup_inputs(seed: int=0):
    np.random.seed(seed)
    _w = jnp.asarray

    def _L0_attn_setup():
        import jax, jax.numpy as jnp
        import numpy as np
        B_, L_, D_, N_ = (4, 512, 128, 32)
        key = jax.random.key(seed)
        ks = jax.random.split(key, 8)

        def n(k, shape, s=0.02):
            return jax.random.normal(k, shape, jnp.float32) * s
        return {'x': jax.random.normal(ks[0], (B_, L_, D_), jnp.float32), 'in_w': n(ks[1], (2 * D_, D_)), 'in_b': jnp.zeros((2 * D_,), jnp.float32), 'conv_w': n(ks[2], (D_, 1, 4), 0.1), 'conv_b': jnp.zeros((D_,), jnp.float32), 'A_log': -2.0 + 0.1 * jax.random.normal(ks[3], (D_, N_), jnp.float32), 'B_w': n(ks[4], (N_, D_)), 'B_b': jnp.zeros((N_,), jnp.float32), 'C_w': n(ks[5], (N_, D_)), 'C_b': jnp.zeros((N_,), jnp.float32), 'out_w': n(ks[6], (D_, D_)), 'out_b': jnp.zeros((D_,), jnp.float32), 'ln_w': jnp.ones((D_,), jnp.float32), 'ln_b': jnp.zeros((D_,), jnp.float32)}
    _L0_attn_in = _L0_attn_setup()

    def _L0_ffn_setup():
        import jax, jax.numpy as jnp
        import numpy as np
        B, S, D, E, F = (2, 256, 128, 8, 512)
        key = jax.random.key(seed)
        ks = jax.random.split(key, 4)
        return {'hidden_states': jax.random.normal(ks[0], (B, S, D), dtype=jnp.float32), 'Wr': jax.random.normal(ks[1], (D, E), dtype=jnp.float32) * (1.0 / np.sqrt(D)), 'W1': jax.random.normal(ks[2], (E, D, F), dtype=jnp.float32) * (1.0 / np.sqrt(D)), 'b1': jnp.zeros((E, F), dtype=jnp.float32), 'W2': jax.random.normal(ks[3], (E, F, D), dtype=jnp.float32) * (1.0 / np.sqrt(F)), 'b2': jnp.zeros((E, D), dtype=jnp.float32)}
    _L0_ffn_in = _L0_ffn_setup()
    _d = {'L0_attn_x': _L0_attn_in['x'], 'L0_attn_in_w': _L0_attn_in['in_w'], 'L0_attn_in_b': _L0_attn_in['in_b'], 'L0_attn_conv_w': _L0_attn_in['conv_w'], 'L0_attn_conv_b': _L0_attn_in['conv_b'], 'L0_attn_A_log': _L0_attn_in['A_log'], 'L0_attn_B_w': _L0_attn_in['B_w'], 'L0_attn_B_b': _L0_attn_in['B_b'], 'L0_attn_C_w': _L0_attn_in['C_w'], 'L0_attn_C_b': _L0_attn_in['C_b'], 'L0_attn_out_w': _L0_attn_in['out_w'], 'L0_attn_out_b': _L0_attn_in['out_b'], 'L0_attn_ln_w': _L0_attn_in['ln_w'], 'L0_attn_ln_b': _L0_attn_in['ln_b'], 'L0_ffn_Wr': _L0_ffn_in['Wr'], 'L0_ffn_W1': _L0_ffn_in['W1'], 'L0_ffn_b1': _L0_ffn_in['b1'], 'L0_ffn_W2': _L0_ffn_in['W2'], 'L0_ffn_b2': _L0_ffn_in['b2']}
    _x0 = _d['L0_attn_x']
    _d['L0_attn_x'] = jax.random.normal(jax.random.fold_in(jax.random.key(seed), 1), (8, 512, 128), dtype=_x0.dtype)
    del _x0
    return _d

def reference(L0_attn_x, L0_attn_in_w, L0_attn_in_b, L0_attn_conv_w, L0_attn_conv_b, L0_attn_A_log, L0_attn_B_w, L0_attn_B_b, L0_attn_C_w, L0_attn_C_b, L0_attn_out_w, L0_attn_out_b, L0_attn_ln_w, L0_attn_ln_b, L0_ffn_Wr, L0_ffn_W1, L0_ffn_b1, L0_ffn_W2, L0_ffn_b2):

    def _L0_attn_ref(x, in_w, in_b, conv_w, conv_b, A_log, B_w, B_b, C_w, C_b, out_w, out_b, ln_w, ln_b):
        import jax, jax.numpy as jnp
        import numpy as np
        B_, L_, D_, N_ = (4, 512, 128, 32)
        Bsz, L, D = x.shape
        residual = x
        xz = x @ in_w.T + in_b
        xa, z = (xz[..., :D], xz[..., D:])
        xc = jax.lax.conv_general_dilated(xa.transpose(0, 2, 1), conv_w, (1,), [(2, 2)], feature_group_count=D, dimension_numbers=('NCH', 'OIH', 'NCH'))
        xc = xc + conv_b[None, :, None]
        xc = jax.nn.silu(xc.transpose(0, 2, 1))
        A = -jnp.exp(jnp.clip(A_log, -5.0, 2.0))
        Bm = xc @ B_w.T + B_b
        Cm = xc @ C_w.T + C_b
        xs = (xc[:, :L].transpose(1, 0, 2), Bm[:, :L].transpose(1, 0, 2), Cm[:, :L].transpose(1, 0, 2))
        s0 = jnp.zeros((Bsz, D, A.shape[1]), x.dtype)

        def step(s, t):
            x_t, b_t, c_t = t
            s = jnp.clip(s * A + b_t[:, None, :] * x_t[:, :, None], -10.0, 10.0)
            y = jnp.sum(c_t[:, None, :] * s, axis=-1)
            return (s, y)
        _, ys = jax.lax.scan(step, s0, xs)
        y = ys.transpose(1, 0, 2) * jax.nn.silu(z)
        out = y @ out_w.T + out_b
        h = out + residual
        mu = jnp.mean(h, axis=-1, keepdims=True)
        var = jnp.var(h, axis=-1, keepdims=True)
        return (h - mu) / jnp.sqrt(var + 1e-05) * ln_w + ln_b

    def _L0_ffn_ref(hidden_states, Wr, W1, b1, W2, b2):
        import jax, jax.numpy as jnp
        import numpy as np
        B, S, D, E, F = (2, 256, 128, 8, 512)
        b, s, d = hidden_states.shape
        e = Wr.shape[1]
        x = hidden_states.reshape(b * s, d)
        router_logits = x @ Wr
        router_probs = jax.nn.softmax(router_logits, axis=-1)
        expert_idx = jnp.argmax(router_probs, axis=-1)
        p_max = jnp.max(router_probs, axis=-1, keepdims=True)

        def expert_mlp(w1, bb1, w2, bb2):
            h = jax.nn.gelu(x @ w1 + bb1, approximate=False)
            return h @ w2 + bb2
        outs = jax.vmap(expert_mlp)(W1, b1, W2, b2)
        onehot = jax.nn.one_hot(expert_idx, e, dtype=x.dtype)
        next_states = jnp.einsum('te,etd->td', onehot, outs)
        out = p_max * next_states
        return out.reshape(b, s, d)
    x = L0_attn_x
    x = x + 0.5 * _L0_ffn_ref(_layernorm(x, axis=-1), L0_ffn_Wr, L0_ffn_W1, L0_ffn_b1, L0_ffn_W2, L0_ffn_b2)
    x = x + _L0_attn_ref(_layernorm(x, axis=-1), L0_attn_in_w, L0_attn_in_b, L0_attn_conv_w, L0_attn_conv_b, L0_attn_A_log, L0_attn_B_w, L0_attn_B_b, L0_attn_C_w, L0_attn_C_b, L0_attn_out_w, L0_attn_out_b, L0_attn_ln_w, L0_attn_ln_b)
    x = x + 0.5 * _L0_ffn_ref(_layernorm(x, axis=-1), L0_ffn_Wr, L0_ffn_W1, L0_ffn_b1, L0_ffn_W2, L0_ffn_b2)
    return x

_drawn_inputs = setup_inputs


def setup_inputs(seed=0):
    import zlib

    import numpy as np

    out = dict(_drawn_inputs(seed))
    spreads = {'L0_attn_in_b': (0.0, 0.8),
     'L0_attn_conv_b': (0.0, 0.8),
     'L0_attn_B_b': (0.0, 0.8),
     'L0_attn_C_b': (0.0, 0.8),
     'L0_attn_out_b': (0.0, 0.1),
     'L0_attn_ln_w': (1.0, 0.2),
     'L0_attn_ln_b': (0.0, 0.1),
     'L0_ffn_b1': (0.0, 0.41),
     'L0_ffn_b2': (0.0, 0.283)}
    factors = {'L0_attn_in_w': 8.0,
     'L0_attn_conv_w': 8.0,
     'L0_attn_A_log': 8.0,
     'L0_attn_B_w': 8.0,
     'L0_attn_C_w': 8.0,
     'L0_attn_out_w': 8.0}
    for name, (base, spread) in spreads.items():
        noise = np.random.default_rng([zlib.crc32(name.encode()), seed]).standard_normal(out[name].shape)
        drawn = base * np.exp(spread * noise) if base else spread * noise
        out[name] = jnp.asarray(drawn.astype(out[name].dtype))
    for name, factor in factors.items():
        out[name] = (out[name] * factor).astype(out[name].dtype)
    return out
```

```python
from contextlib import ExitStack

import concourse.bass as bass
from concourse import mybir

F32 = mybir.dt.float32
I32 = mybir.dt.int32
U32 = mybir.dt.uint32
ALU = mybir.AluOpType
ACT = mybir.ActivationFunctionType
AX = mybir.AxisListType

P = 128
BATCH, L, D = 8, 512, 128
TOK = BATCH * L
NT = TOK // P
E, F = 8, 512
FC = F // P
ST = 32
TILES = 40
SLOTS = TILES * P
ROW = D + 1
EPS = 1e-5
WROW = FC * P + FC * P + FC + D
W2_AT, B1_AT, B2_AT = F, 2 * F, 2 * F + FC
Q = 4
CH = 64
NCH = L // CH
GRP = 2
HALF = BATCH // GRP * ST
QUADS = L // Q


def spread(ap, dims):
    return bass.AP(tensor=ap.tensor, offset=ap.offset, ap=[list(ap.ap[0])] + [list(d) for d in dims])


class Tensors:
    pass


def build(nc, a, out):
    with ExitStack() as ctx:
        def sb(name, shape, dt=F32):
            return ctx.enter_context(nc.sbuf_tensor(name, shape, dt))

        def dram(name, shape):
            return nc.dram_tensor(name, shape, F32, kind="Internal").ap()

        T = Tensors()
        T.x = sb("x", [P, NT, D])
        T.xn = sb("xn", [P, NT, ROW])
        T.xt = sb("xt", [P, TOK])
        T.tables = sb("tables", [P, E, WROW])
        T.ident = sb("ident", [P, P])
        T.before = sb("before", [P, P])
        T.ones = sb("ones", [P, P])
        T.wr = sb("wr", [P, E])
        T.tile_expert = sb("tile_expert", [P, TILES], I32)
        T.slot = sb("slot", [P, NT], U32)
        T.gate = sb("gate", [P, NT])
        T.rstd = sb("rstd", [P, NT])
        T.stat = sb("stat", [P, NT, 2])
        T.share = sb("share", [P, 2 * CH // Q * BATCH * ST])
        T.in_t = sb("in_t", [P, 2 * D])
        T.b_t = sb("b_t", [P, ST])
        T.c_rep = sb("c_rep", [P, Q, ST])
        T.o_q = sb("o_q", [P, Q, D])
        T.conv_diag = sb("conv_diag", [P, Q, P])
        T.cols = sb("cols", [P, 3 + Q])
        T.rows = sb("rows", [P, 3, D])
        T.bb_row = sb("bb_row", [P, ST])
        T.decay = sb("decay", [P, ST])
        T.mask4 = sb("mask4", [P, Q])
        T.mask8 = sb("mask8", [P, BATCH])
        T.mask16 = sb("mask16", [P, Q * Q])
        T.stack = sb("stack", [P, ST])
        T.zq = sb("zq", [P, GRP, Q, L])
        T.xa = sb("xa", [P, BATCH, L + 4])
        T.sorted = [dram(f"sorted{n}", [SLOTS, ROW]) for n in range(2)]
        T.ffn_out = [dram(f"ffn_out{n}", [TOK + SLOTS, D]) for n in range(2)]
        T.bank = [ctx.enter_context(nc.psum_tensor(f"bank{n}", [P, 512], F32)) for n in range(8)]

        setup(nc, T, a)
        for n in range(2):
            normalize(nc, T, f"n{n}_", T.x, logits=True)
            route(nc, T, f"r{n}_", T.sorted[n])
            experts(nc, T, f"e{n}_", T.sorted[n], T.ffn_out[n])
            combine(nc, T, f"c{n}_", T.ffn_out[n], out if n else None)
            if n == 0:
                normalize(nc, T, "nb_", T.x)
                project_in(nc, T)
                scan(nc, T)
                project_out(nc, T)
                normalize(nc, T, "no_", T.xn, turn=False)
                add_normalized(nc, T)
    return nc


def setup(nc, T, a):
    with ExitStack() as ctx:
        def sem(name):
            return ctx.enter_context(nc.semaphore("s_" + name))

        def sb(name, shape, dt=F32):
            return ctx.enter_context(nc.sbuf_tensor("s_" + name, shape, dt))

        x_in, w_in, tables_in, small_in, pads_out = map(sem, ("x_in", "w_in", "tables_in", "small_in", "pads_out"))
        pool_made, dve_made, pe_made, act_made = map(sem, ("pool_made", "dve_made", "pe_made", "act_made"))
        in_w = sb("in_w", [P, 2, D])
        bc_w = sb("bc_w", [2 * ST, D])
        out_w = sb("out_w", [P, D])
        b1 = sb("b1", [E * FC, P])
        taps = sb("taps", [P, Q])
        a_log = sb("a_log", [P, ST])
        a_t = sb("a_t", [P, ST])
        fill = T.share[:, 0:TILES * ROW].rearrange("p (i r) -> p i r", r=ROW)

        with nc.Block() as block:
            @block.sync
            def _(sp):
                sp.dma_start(T.x[:], a["L0_attn_x"].rearrange("b (q p) d -> p (b q) d", p=P)).then_inc(x_in, 16)
                sp.dma_start(T.wr[:], a["L0_ffn_Wr"]).then_inc(w_in, 16)
                sp.dma_start(in_w[:], a["L0_attn_in_w"].rearrange("(h p) c -> p h c", p=P)).then_inc(w_in, 16)
                sp.dma_start(bc_w[0:ST, :], a["L0_attn_B_w"]).then_inc(w_in, 16)
                sp.dma_start(bc_w[ST:2 * ST, :], a["L0_attn_C_w"]).then_inc(w_in, 16)
                sp.dma_start(out_w[:], a["L0_attn_out_w"]).then_inc(w_in, 16)
                sp.dma_start(b1[:], a["L0_ffn_b1"].rearrange("e (c p) -> (e c) p", p=P)).then_inc(w_in, 16)
                sp.dma_start(taps[:], a["L0_attn_conv_w"].rearrange("c o k -> c (o k)")).then_inc(w_in, 16)
                sp.dma_start(a_log[:], a["L0_attn_A_log"]).then_inc(w_in, 16)
                sp.dma_start(T.tables[:, :, 0:F], a["L0_ffn_W1"].rearrange("e d f -> d e f")).then_inc(tables_in, 16)
                for e in range(E):
                    sp.dma_start(T.tables[:, e, W2_AT:W2_AT + F].rearrange("p (c d) -> p c d", d=D),
                                 a["L0_ffn_W2"][e].rearrange("(c p) d -> p c d", p=P)).then_inc(tables_in, 16)
                sp.wait_ge(pool_made, 4)
                for n in range(2):
                    sp.dma_start(T.sorted[n].rearrange("(i p) r -> p i r", p=P), fill).then_inc(pads_out, 16)
                sp.wait_ge(pads_out, 32)
                sp.wait_ge(tables_in, 16 * (1 + E))
                sp.wait_ge(x_in, 16)

            @block.scalar
            def _(act):
                for k, name in enumerate(("L0_attn_out_b", "L0_attn_ln_w", "L0_attn_ln_b")):
                    act.dma_start(T.rows[:, k, :], bass.AP(tensor=a[name].tensor, offset=0, ap=[[0, P], [1, D]])).then_inc(small_in, 16)
                act.dma_start(T.bb_row[:], bass.AP(tensor=a["L0_attn_B_b"].tensor, offset=0, ap=[[0, P], [1, ST]])).then_inc(small_in, 16)
                act.dma_start(T.tables[:, :, B2_AT:B2_AT + D],
                              bass.AP(tensor=a["L0_ffn_b2"].tensor, offset=0, ap=[[0, P], [D, E], [1, D]])).then_inc(small_in, 16)
                column = lambda name, at, step=1, n=P: bass.AP(tensor=a[name].tensor, offset=at, ap=[[step, n], [1, 1]])
                act.dma_start(T.cols[:, 0:1], column("L0_attn_in_b", 0)).then_inc(small_in, 16)
                act.dma_start(T.cols[:, 1:2], column("L0_attn_conv_b", 0)).then_inc(small_in, 16)
                for b in range(Q):
                    rows = slice(ST * b, ST * b + ST)
                    act.dma_start(T.cols[rows, 2:3], column("L0_attn_C_b", 0, n=ST)).then_inc(small_in, 16)
                    for dq in range(Q):
                        act.dma_start(T.cols[rows, 3 + dq:4 + dq], column("L0_attn_in_b", D + dq * ST, n=ST)).then_inc(small_in, 16)
                act.wait_ge(dve_made, 2)
                act.activation(T.decay[:], a_t[:], ACT.Exp).then_inc(act_made, 1)
                act.wait_ge(small_in, 16 * (7 + Q * (1 + Q)))

            @block.gpsimd
            def _(pool):
                pool.memset(T.ones[:], 1.0).then_inc(pool_made, 1)
                pool.memset(fill[:, :, 0:D], 0.0).then_inc(pool_made, 1)
                pool.iota(fill.bitcast(I32)[:, :, D:ROW], pattern=[[P, TILES]], base=TOK, channel_multiplier=1).then_inc(pool_made, 1)
                pool.iota(T.xn[:].bitcast(I32)[:, :, D:ROW], pattern=[[P, NT]], base=0, channel_multiplier=1).then_inc(pool_made, 1)
                pool.wait_ge(pool_made, 1)
                pool.affine_select(out=T.ident[:], in_=T.ones[:], compare_op=ALU.is_equal, fill=0.0,
                                   base=0, pattern=[[-1, P]], channel_multiplier=1).then_inc(pool_made, 1)
                pool.affine_select(out=T.before[:], in_=T.ones[:], compare_op=ALU.is_gt, fill=0.0,
                                   base=0, pattern=[[1, P]], channel_multiplier=-1).then_inc(pool_made, 1)
                pool.memset(T.xa[:], 0.0).then_inc(pool_made, 1)

            @block.vector
            def _(dve):
                dve.wait_ge(w_in, 16 * 8)
                dve.tensor_scalar(a_log[:], a_log[:], -5.0, 2.0, ALU.max, ALU.min).then_inc(dve_made, 1)
                dve.wait_ge(dve_made, 1)
                dve.transpose(a_t[:], a_log[:]).then_inc(dve_made, 1)
                dve.wait_ge(pool_made, 7)
                ident = T.ident[:]
                dve.tensor_reduce(T.mask4[:], ident.rearrange("p (i k) -> p i k", i=Q), AX.X, ALU.add).then_inc(dve_made, 1)
                dve.tensor_reduce(T.mask16[:], ident.rearrange("p (i k) -> p i k", i=Q * Q), AX.X, ALU.add).then_inc(dve_made, 1)
                dve.tensor_reduce(T.mask8[:], ident.rearrange("p (k i) -> p i k", i=BATCH), AX.X, ALU.add).then_inc(dve_made, 1)
                dve.tensor_reduce(T.stack[:], ident.rearrange("p (k i) -> p i k", i=ST), AX.X, ALU.add).then_inc(dve_made, 1)
                for k in range(Q):
                    dve.tensor_scalar(T.conv_diag[:, k, :], ident, taps[:, k:k + 1], None, ALU.mult).then_inc(dve_made, 1)
                dve.wait_ge(pe_made, 1)
                dve.tensor_copy(T.in_t[:], T.bank[0][:, 0:2 * D]).then_inc(dve_made, 1)
                dve.tensor_copy(T.b_t[:], T.bank[1][:, 0:ST]).then_inc(dve_made, 1)
                dve.tensor_copy(T.c_rep[:], spread(T.bank[1][:, ST:2 * ST], [[0, Q], [1, ST]])).then_inc(dve_made, 1)
                dve.tensor_copy(T.tables[:, :, B1_AT:B1_AT + FC],
                                T.bank[2][:, 0:E * FC].rearrange("p (e c) -> p e c", c=FC)).then_inc(dve_made, 1)
                dve.tensor_copy(T.o_q[:], T.bank[3][:, 0:Q * D].rearrange("p (q d) -> p q d", d=D)).then_inc(dve_made, 1)
                dve.wait_ge(act_made, 1)
                dve.tensor_scalar(T.decay[:], T.decay[:], -1.0, None, ALU.mult).then_inc(dve_made, 1)

            @block.tensor
            def _(pe):
                pe.wait_ge(w_in, 16 * 8)
                pe.wait_ge(pool_made, 7)
                for h in range(2):
                    pe.transpose(T.bank[0][:, h * D:(h + 1) * D], in_w[:, h, :], T.ident[:])
                pe.transpose(T.bank[1][:, 0:2 * ST], bc_w[:], T.ident[0:2 * ST, 0:2 * ST])
                pe.transpose(T.bank[2][:, 0:E * FC], b1[:], T.ident[0:E * FC, 0:E * FC])
                for b in range(Q):
                    for dq in range(Q):
                        last = pe.matmul(T.bank[3][ST * b:ST * b + ST, dq * D:(dq + 1) * D],
                                         out_w[:, dq * ST:(dq + 1) * ST], T.ident[:], start=True, stop=True)
                last.then_inc(pe_made, 1)


def normalize(nc, T, tag, src, turn=True, logits=False):
    with ExitStack() as ctx:
        def sem(name):
            return ctx.enter_context(nc.semaphore(tag + name))

        def sb(name, shape, dt=F32):
            return ctx.enter_context(nc.sbuf_tensor(tag + name, shape, dt))

        stats_made, aggregated, chain, root_made, normed, transposed, xt_made = map(
            sem, ("stats_made", "aggregated", "chain", "root_made", "normed", "transposed", "xt_made"))
        raw = sb("raw", [P, NT, 6])
        var = sb("var", [P, NT])
        tmp = sb("tmp", [P, NT])
        with nc.Block() as block:
            @block.vector
            def _(dve):
                for j in range(NT):
                    dve.bn_stats(raw[:, j, :], src[:, j, 0:D]).then_inc(stats_made, 1)
                for j in range(NT):
                    dve.wait_ge(stats_made, j + 1)
                    dve.bn_aggr(T.stat[:, j, :], raw[:, j, :]).then_inc(aggregated, 1)
                dve.wait_ge(aggregated, NT)
                dve.tensor_scalar(var[:], T.stat[:, :, 1], EPS, None, ALU.add).then_inc(chain, 1)
                dve.wait_ge(root_made, 1)
                dve.reciprocal(T.rstd[:], tmp[:]).then_inc(chain, 1)
                dve.wait_ge(chain, 2)
                dve.tensor_tensor(tmp[:], T.rstd[:], T.rstd[:], ALU.mult).then_inc(chain, 1)
                dve.wait_ge(chain, 3)
                dve.tensor_tensor(tmp[:], tmp[:], var[:], ALU.mult).then_inc(chain, 1)
                dve.wait_ge(chain, 4)
                dve.tensor_scalar(tmp[:], tmp[:], -0.5, 1.5, ALU.mult, ALU.add).then_inc(chain, 1)
                dve.wait_ge(chain, 5)
                dve.tensor_tensor(T.rstd[:], T.rstd[:], tmp[:], ALU.mult).then_inc(chain, 1)
                dve.wait_ge(chain, 6)
                for j in range(NT):
                    dve.tensor_scalar(T.xn[:, j, 0:D], src[:, j, 0:D], T.stat[:, j, 0:1], T.rstd[:, j:j + 1],
                                      ALU.subtract, ALU.mult).then_inc(normed, 1)

            @block.scalar
            def _(act):
                act.wait_ge(chain, 1)
                act.activation(tmp[:], var[:], ACT.Sqrt).then_inc(root_made, 1)
                for g in range(NT // 4 if turn else 0):
                    act.wait_ge(transposed, g + 1)
                    act.activation(T.xt[:, g * 512:(g + 1) * 512], T.bank[g % 2][:], ACT.Copy).then_inc(xt_made, 1)

            @block.tensor
            def _(pe):
                for g in range(NT // 4 + 1 if turn else 0):
                    if g < NT // 4:
                        if g >= 2:
                            pe.wait_ge(xt_made, g - 1)
                        for j in range(4 * g, 4 * g + 4):
                            pe.wait_ge(normed, j + 1)
                            last = pe.transpose(T.bank[g % 2][:, (j % 4) * P:(j % 4 + 1) * P], T.xn[:, j, 0:D], T.ident[:])
                        last.then_inc(transposed, 1)
                    if g >= 1 and logits:
                        pe.wait_ge(xt_made, g)
                        for j in range(4 * g - 4, 4 * g):
                            pe.matmul(T.bank[2][:, j * E:(j + 1) * E], T.xt[:, j * P:(j + 1) * P], T.wr[:],
                                      start=True, stop=True)


def route(nc, T, tag, sorted_rows):
    with ExitStack() as ctx:
        def sem(name):
            return ctx.enter_context(nc.semaphore(tag + name))

        def sb(name, shape, dt=F32):
            return ctx.enter_context(nc.sbuf_tensor(tag + name, shape, dt))

        chain, exps_made, counted, const_made, scattered = map(
            sem, ("chain", "exps_made", "counted", "const_made", "scattered"))
        logits = sb("logits", [P, E, NT])
        exps = sb("exps", [P, E, NT])
        pick = sb("pick", [P, E, NT])
        place = sb("place", [P, E, NT])
        upto = sb("upto", [P, E, NT])
        carry = sb("carry", [P, E, NT])
        best = sb("best", [P, NT])
        total = sb("total", [P, NT])
        rank_e = sb("rank_e", [P, E])
        count = sb("count", [P, E], I32)
        tiles = sb("tiles", [P, E])
        ends = sb("ends", [P, E])
        base = sb("base", [P, E])
        tile_no = sb("tile_no", [P, TILES])
        past = sb("past", [P, TILES, E])
        tile_e = sb("tile_e", [P, TILES])

        by_tile = lambda t: t[:].rearrange("p e j -> p j e")
        over_e = lambda t: spread(t[:], [[0, E], [1, NT]])
        over_j = lambda t: spread(t[:], [[1, E], [0, NT]])

        with nc.Block() as block:
            @block.gpsimd
            def _(pool):
                pool.memset(carry[:], 1.0).then_inc(const_made, 1)
                pool.iota(rank_e[:], pattern=[[-1, E]], base=E, channel_multiplier=0,
                          allow_small_or_imprecise_dtypes=True).then_inc(const_made, 1)
                pool.iota(tile_no[:], pattern=[[1, TILES]], base=0, channel_multiplier=0,
                          allow_small_or_imprecise_dtypes=True).then_inc(const_made, 1)
                pool.wait_ge(const_made, 3)
                pool.memset(carry[:, :, 0:1], 0.0).then_inc(const_made, 1)
                pool.wait_ge(chain, 25)
                for j in range(NT):
                    pool.indirect_dma_start(sorted_rows, bass.IndirectOffsetOnAxis(ap=T.slot[:, j:j + 1], axis=0),
                                            T.xn[:, j, :], None).then_inc(scattered, 16)
                pool.wait_ge(scattered, 16 * NT)

            @block.scalar
            def _(act):
                act.wait_ge(chain, 3)
                act.activation(exps[:], logits[:], ACT.Exp).then_inc(exps_made, 1)

            @block.tensor
            def _(pe):
                pe.wait_ge(chain, 7)
                pe.matmul(T.bank[0][:, 0:E * NT], T.before[:], pick[:].rearrange("p e j -> p (e j)"), start=True, stop=True)
                pe.matmul(T.bank[1][:, 0:E * NT], T.ones[:], pick[:].rearrange("p e j -> p (e j)"),
                          start=True, stop=True).then_inc(counted, 1)

            @block.vector
            def _(dve):
                done = [0]

                def then(instruction):
                    done[0] += 1
                    instruction.then_inc(chain, 1)
                    dve.wait_ge(chain, done[0])

                then(dve.tensor_copy(logits[:], T.bank[2][:, 0:E * NT].rearrange("p (j e) -> p e j", e=E)))
                then(dve.tensor_reduce(best[:], by_tile(logits), AX.X, ALU.max))
                then(dve.tensor_tensor(logits[:], logits[:], over_e(best), ALU.subtract))
                then(dve.tensor_scalar(pick[:], logits[:], 0.0, None, ALU.is_equal))
                dve.wait_ge(const_made, 4)
                then(dve.tensor_tensor(pick[:], pick[:], over_j(rank_e), ALU.mult))
                then(dve.tensor_reduce(best[:], by_tile(pick), AX.X, ALU.max))
                then(dve.tensor_tensor(pick[:], pick[:], over_e(best), ALU.is_equal))
                dve.wait_ge(exps_made, 1)
                then(dve.tensor_reduce(total[:], by_tile(exps), AX.X, ALU.add))
                then(dve.reciprocal(T.gate[:], total[:]))
                then(dve.tensor_scalar(T.gate[:], T.gate[:], 0.5, None, ALU.mult))
                dve.wait_ge(counted, 1)
                flat = lambda t: t[:].rearrange("p e j -> p (e j)")
                then(dve.tensor_tensor_scan(flat(upto), flat(carry), T.bank[1][:, 0:E * NT], 0.0, ALU.mult, ALU.add))
                then(dve.tensor_tensor(flat(place), flat(upto), T.bank[1][:, 0:E * NT], ALU.subtract))
                then(dve.tensor_tensor(flat(place), flat(place), T.bank[0][:, 0:E * NT], ALU.add))
                then(dve.tensor_scalar(count[:], upto[:, :, NT - 1], float(P - 1), None, ALU.add))
                then(dve.tensor_scalar(count[:], count[:], P.bit_length() - 1, None, ALU.arith_shift_right))
                then(dve.tensor_copy(tiles[:], count[:]))
                then(dve.tensor_tensor_scan(ends[:], T.ones[:, 0:E], tiles[:], 0.0, ALU.mult, ALU.add))
                then(dve.tensor_tensor(base[:], ends[:], tiles[:], ALU.subtract))
                then(dve.tensor_scalar(base[:], base[:], float(P), None, ALU.mult))
                then(dve.tensor_tensor(place[:], place[:], over_j(base), ALU.add))
                then(dve.tensor_tensor(place[:], place[:], pick[:], ALU.mult))
                then(dve.tensor_tensor(past[:], spread(tile_no[:], [[1, TILES], [0, E]]),
                                       spread(ends[:], [[0, TILES], [1, E]]), ALU.is_ge))
                then(dve.tensor_reduce(best[:], by_tile(place), AX.X, ALU.add))
                then(dve.tensor_reduce(tile_e[:], past[:], AX.X, ALU.add))
                then(dve.tensor_copy(T.slot[:], best[:]))
                then(dve.tensor_scalar(T.tile_expert[:], tile_e[:], float(E - 1), None, ALU.min))


def experts(nc, T, tag, sorted_rows, ffn_out):
    RING, STAGES = 4, TILES // 4
    with ExitStack() as ctx:
        def sem(name):
            return ctx.enter_context(nc.semaphore(tag + name))

        def sb(name, shape, dt=F32):
            return ctx.enter_context(nc.sbuf_tensor(tag + name, shape, dt))

        loaded = [sem(f"loaded{r}") for r in range(RING)]
        stored = [sem(f"stored{r}") for r in range(RING)]
        turned, x_made, w_made, up_made, h_made, down_made, out_made = map(
            sem, ("turned", "x_made", "w_made", "up_made", "h_made", "down_made", "out_made"))
        rows = [sb(f"rows{r}", [P, ROW]) for r in range(RING)]
        outs = [sb(f"outs{r}", [P, D]) for r in range(RING)]
        xt = [sb(f"xt{r}", [P, P]) for r in range(2)]
        weights = [sb(f"weights{r}", [P, WROW]) for r in range(2)]
        hidden = [sb(f"hidden{r}", [P, FC, P]) for r in range(2)]
        turn, up, down = T.bank[0:2], T.bank[2:4], T.bank[4:6]

        def stages(eng, stage):
            stage(0, True, False)
            with eng.Fori(1, STAGES - 1) as s:
                stage(s, False, False)
            stage(STAGES - 1, False, True)

        with nc.Block() as block:
            @block.sync
            def _(sp):
                def load(s, r):
                    if not isinstance(s, int) or s:
                        sp.wait_ge(stored[r], s * 16)
                    sp.dma_start(rows[r][:], sorted_rows[bass.ds((s * RING + r) * P, P), :]).then_inc(loaded[r], 16)

                for r in range(RING):
                    load(0, r)
                with sp.Fori(1, STAGES) as s:
                    for r in range(RING):
                        load(s, r)

            @block.tensor
            def _(pe):
                def turn_in(s, r, i):
                    pe.wait_ge(loaded[r], (s + 1) * 16)
                    if not (isinstance(i, int) and i < 2):
                        pe.wait_ge(x_made, i - 1)
                    pe.transpose(turn[r % 2][:, 0:P], rows[r][:, 0:D], T.ident[:]).then_inc(turned, 1)

                def go_up(i, r):
                    pe.wait_ge(x_made, i + 1)
                    pe.wait_ge(w_made, i + 1)
                    if not (isinstance(i, int) and i < 2):
                        pe.wait_ge(h_made, i - 1)
                    for c in range(FC):
                        last = pe.matmul(up[r % 2][:, c * P:(c + 1) * P], weights[r % 2][:, c * P:(c + 1) * P], xt[r % 2][:],
                                         start=True, stop=True)
                    last.then_inc(up_made, 1)

                def go_down(i, r):
                    pe.wait_ge(h_made, i + 1)
                    if not (isinstance(i, int) and i < 2):
                        pe.wait_ge(out_made, i - 1)
                    for c in range(FC):
                        last = pe.matmul(down[r % 2][:, 0:D], hidden[r % 2][:, c, :],
                                         weights[r % 2][:, W2_AT + c * D:W2_AT + (c + 1) * D],
                                         start=(c == 0), stop=(c == FC - 1))
                    last.then_inc(down_made, 1)

                def stage(s, first, last):
                    for r in range(RING):
                        i = s * RING + r
                        if not (last and r == RING - 1):
                            turn_in(s + (r + 1) // RING, (r + 1) % RING, i + 1)
                        go_up(i, r)
                        if not (first and r == 0):
                            go_down(i - 1, r - 1)

                turn_in(0, 0, 0)
                stages(pe, stage)
                go_down(TILES - 1, RING - 1)

            @block.scalar
            def _(act):
                with act.Fori(0, STAGES) as s:
                    for r in range(RING):
                        act.wait_ge(up_made, s * RING + r + 1)
                        for c in range(FC):
                            last = act.activation(hidden[r % 2][:, c, :], up[r % 2][:, c * P:(c + 1) * P], ACT.Gelu,
                                                  bias=weights[r % 2][:, B1_AT + c:B1_AT + c + 1])
                        last.then_inc(h_made, 1)

            @block.vector
            def _(dve):
                def take_weights(i, r):
                    e = dve.value_load(T.tile_expert[0:1, bass.ds(i, 1)], min_val=0, max_val=E - 1)
                    if not (isinstance(i, int) and i < 2):
                        dve.wait_ge(down_made, i - 1)
                        dve.wait_ge(out_made, i - 1)
                    flat = T.tables[:].rearrange("p e w -> p (e w)")
                    dve.tensor_copy(weights[r % 2][:], flat[:, bass.ds(e * WROW, WROW)]).then_inc(w_made, 1)

                def take_x(i, r):
                    dve.wait_ge(turned, i + 1)
                    dve.tensor_copy(xt[r % 2][:], turn[r % 2][:, 0:P]).then_inc(x_made, 1)

                def give_out(s, i, r):
                    dve.wait_ge(down_made, i + 1)
                    if not isinstance(s, int) or s:
                        dve.wait_ge(stored[r % RING], s * 16)
                    dve.tensor_tensor(outs[r % RING][:], down[r % 2][:, 0:D],
                                      weights[r % 2][:, B2_AT:B2_AT + D], ALU.add).then_inc(out_made, 1)

                take_weights(0, 0)
                take_x(0, 0)

                def stage(s, first, last):
                    for r in range(RING):
                        i = s * RING + r
                        if not (first and r == 0):
                            give_out(s - (r == 0), i - 1, (r - 1) % RING)
                        if not (last and r == RING - 1):
                            take_weights(i + 1, r + 1)
                            take_x(i + 1, r + 1)

                stages(dve, stage)
                give_out(STAGES - 1, TILES - 1, RING - 1)

            @block.gpsimd
            def _(pool):
                for s in range(STAGES):
                    for r in range(RING):
                        pool.wait_ge(out_made, s * RING + r + 1)
                        pool.indirect_dma_start(ffn_out, bass.IndirectOffsetOnAxis(ap=rows[r][:, D:ROW].bitcast(U32), axis=0),
                                                outs[r][:], None).then_inc(stored[r], 16)
                for r in range(RING):
                    pool.wait_ge(stored[r], 16 * STAGES)


def combine(nc, T, tag, ffn_out, out):
    PARTS = 4
    with ExitStack() as ctx:
        def sem(name):
            return ctx.enter_context(nc.semaphore(tag + name))

        loaded = [sem(f"loaded{n}") for n in range(PARTS)]
        added, stored = sem("added"), sem("stored")
        got = T.share[:, 0:NT * D].rearrange("p (j d) -> p j d", d=D)
        with nc.Block() as block:
            @block.sync
            def _(sp):
                rows = ffn_out[0:TOK, :].rearrange("(j p) d -> p j d", p=P)
                for n in range(PARTS):
                    part = slice(n * NT // PARTS, (n + 1) * NT // PARTS)
                    sp.dma_start(got[:, part, :], rows[:, part, :]).then_inc(loaded[n], 16)
                if out is not None:
                    to = out.rearrange("b (q p) d -> p (b q) d", p=P)
                    for n in range(PARTS):
                        part = slice(n * NT // PARTS, (n + 1) * NT // PARTS)
                        sp.wait_ge(added, (n + 1) * NT // PARTS)
                        sp.dma_start(to[:, part, :], T.x[:, part, :]).then_inc(stored, 16)
                    sp.wait_ge(stored, 16 * PARTS)

            @block.vector
            def _(dve):
                for j in range(NT):
                    if j % (NT // PARTS) == 0:
                        dve.wait_ge(loaded[j * PARTS // NT], 16)
                    dve.scalar_tensor_tensor(T.x[:, j, :], got[:, j, :], T.gate[:, j:j + 1], T.x[:, j, :],
                                             ALU.mult, ALU.add).then_inc(added, 1)


def project_in(nc, T):
    with ExitStack() as ctx:
        made, taken = ctx.enter_context(nc.semaphore("pi_made")), ctx.enter_context(nc.semaphore("pi_taken"))
        with nc.Block() as block:
            @block.tensor
            def _(pe):
                for n in range(2 * BATCH):
                    bank = T.bank[n % 4]
                    if n >= 4:
                        pe.wait_ge(taken, n - 3)
                    if n < BATCH:
                        last = pe.matmul(bank[:], T.in_t[:, 0:D], T.xt[:, n * L:(n + 1) * L], start=True, stop=True)
                    else:
                        half, dq = (n - BATCH) // Q, (n - BATCH) % Q
                        for b in range(Q):
                            at = (half * Q + b) * L
                            last = pe.matmul(bank[ST * b:ST * b + ST, :], T.in_t[:, D + dq * ST:D + (dq + 1) * ST],
                                             T.xt[:, at:at + L], start=True, stop=True)
                    last.then_inc(made, 1)

            @block.scalar
            def _(act):
                for n in range(2 * BATCH):
                    act.wait_ge(made, n + 1)
                    if n < BATCH:
                        act.activation(T.xa[:, n, 2:2 + L], T.bank[n % 4][:], ACT.Identity,
                                       bias=T.cols[:, 0:1]).then_inc(taken, 1)
                    else:
                        half, dq = (n - BATCH) // Q, (n - BATCH) % Q
                        act.activation(T.zq[:, half, dq, :], T.bank[n % 4][:], ACT.Silu,
                                       bias=T.cols[:, 3 + dq:4 + dq]).then_inc(taken, 1)


def scan(nc, T):
    with ExitStack() as ctx:
        def sem(name):
            return ctx.enter_context(nc.semaphore("sc_" + name))

        def sb(name, shape, dt=F32):
            return ctx.enter_context(nc.sbuf_tensor("sc_" + name, shape, dt))

        conv_made, xc_made, xr_made, xq_made, c_product, c_made, b_product, b_taken, x_product, xd_made = map(
            sem, ("conv_made", "xc_made", "xr_made", "xq_made", "c_product", "c_made", "b_product", "b_taken", "x_product", "xd_made"))
        b_biased, wb_made, cb_made, u_made, y_made, y_taken = map(
            sem, ("b_biased", "wb_made", "cb_made", "u_made", "y_made", "y_taken"))
        steps = sem("steps")
        zeroed = sem("zeroed")

        TT = CH // Q
        xc = sb("xc", [P, BATCH, CH])
        xr = sb("xr", [P, CH, Q, BATCH])
        xq = sb("xq", [P, CH, Q, BATCH])
        cr = sb("cr", [P, 2 * CH * BATCH])
        bq = sb("bq", [P, 2 * TT * ST])
        xd = T.share
        wb = [sb(f"wb{h}", [P, Q, P]) for h in range(2)]
        cb = [sb(f"cb{h}", [P, Q, BATCH, Q]) for h in range(2)]
        state = sb("state", [P, 2 * Q, GRP, HALF])
        scaled = sb("scaled", [P, GRP, HALF])
        summed = sb("summed", [P, GRP, HALF])
        ys = T.xt[:].rearrange("p (h q t) -> p h q t", h=GRP, q=Q)
        u_bank, y_bank, prep = T.bank[0:4], T.bank[4:6], T.bank[6:8]

        with nc.Block() as block:
            @block.tensor
            def _(pe):
                def convolve(k):
                    if not (isinstance(k, int) and k == 0):
                        pe.wait_ge(b_taken, k)
                    for tap in range(4):
                        last = pe.matmul(prep[0][:], T.conv_diag[:, tap, :], T.xa[:, :, bass.ds(k * CH + tap, CH)],
                                         start=(tap == 0), stop=(tap == 3))
                    last.then_inc(conv_made, 1)

                def project(k):
                    pe.wait_ge(xc_made, k + 1)
                    if not (isinstance(k, int) and k == 0):
                        pe.wait_ge(xd_made, k)
                    pe.matmul(prep[1][:], T.c_rep[:].rearrange("p q n -> p (q n)"),
                              xc[:].rearrange("p b t -> p t b"), start=True, stop=True).then_inc(c_product, 1)
                    pe.wait_ge(xr_made, k + 1)
                    for tt in range(TT):
                        last = pe.matmul(prep[0][:, tt * ST:(tt + 1) * ST],
                                         xr[:, Q * tt:Q * tt + Q, :, :].rearrange("p t q b -> p (t q b)"), T.b_t[:],
                                         start=True, stop=True)
                    last.then_inc(b_product, 1)

                def regroup(k):
                    pe.wait_ge(xq_made, k + 1)
                    pe.wait_ge(c_made, k + 1)
                    for tt in range(TT):
                        last = pe.matmul(prep[1][:, tt * ST:(tt + 1) * ST],
                                         xq[:, Q * tt:Q * tt + Q, :, :].rearrange("p t q b -> p (t q b)"), T.stack[:],
                                         start=True, stop=True)
                    last.then_inc(x_product, 1)

                def outer(q, h):
                    pe.wait_ge(wb_made, q + 1)
                    for m in range(2):
                        if not (isinstance(q, int) and q < 2):
                            pe.wait_ge(steps, (q * 2 + m - 4) * 12 + 10)
                        for i in range(2):
                            last = pe.matmul(u_bank[2 * h + m][:, i * 256:(i + 1) * 256], wb[h][:, 2 * m + i, :],
                                             xd[:, bass.ds(q % (2 * TT) * 256, 256)], start=True, stop=True)
                        last.then_inc(u_made, 1)

                def contract(q, h):
                    pe.wait_ge(cb_made, q + 1)
                    if not (isinstance(q, int) and q < 2):
                        pe.wait_ge(y_taken, q - 1)
                    for i in range(Q):
                        for half in range(GRP):
                            pe.wait_ge(steps, q * 24 + 6 * i + 5 + half)
                            at = (i * GRP + half) * 16
                            last = pe.matmul(y_bank[h][:, at:at + 16], state[:, Q * h + i, half, :],
                                             cb[h][:, i, half * Q:(half + 1) * Q, :].rearrange("p b q -> p (b q)"),
                                             start=True, stop=True)
                    last.then_inc(y_made, 1)

                def eight_steps(n):
                    for h in range(2):
                        outer(n * 2 + h + 1, (h + 1) % 2)
                        contract(n * 2 + h, h)

                convolve(0)
                project(0)
                regroup(0)
                outer(0, 0)
                convolve(1)
                eight_steps(0)
                project(1)
                eight_steps(1)
                regroup(1)
                with pe.Fori(2, 8) as n:
                    eight_steps(n)
                with pe.Fori(1, NCH - 1) as k:
                    convolve(k + 1)
                    eight_steps(k * 8)
                    project(k + 1)
                    eight_steps(k * 8 + 1)
                    regroup(k + 1)
                    with pe.Fori(2, 8) as n:
                        eight_steps(k * 8 + n)
                with pe.Fori((NCH - 1) * 8, NCH * 8 - 1) as n:
                    eight_steps(n)
                outer(QUADS - 1, 1)
                contract(QUADS - 2, 0)
                contract(QUADS - 1, 1)

            @block.scalar
            def _(act):
                def take_conv(k):
                    act.wait_ge(conv_made, k + 1)
                    act.activation(xc[:].rearrange("p b t -> p (b t)"), prep[0][:], ACT.Silu, bias=T.cols[:, 1:2]).then_inc(xc_made, 1)
                    act.wait_ge(xc_made, k + 1)
                    act.activation(xr[:], spread(xc[:, 0, 0:1], [[1, CH], [0, Q], [CH, BATCH]]), ACT.Copy).then_inc(xr_made, 1)
                    for dq in range(Q):
                        last = act.activation(xq[:, :, dq, :], xc[:].rearrange("p b t -> p t b"), ACT.Copy,
                                              scale=T.mask4[:, dq:dq + 1])
                    last.then_inc(xq_made, 1)

                def take_bc(k):
                    act.wait_ge(c_product, k + 1)
                    act.activation(cr[:, bass.ds(k % 2 * (CH * BATCH), CH * BATCH)], prep[1][:], ACT.Identity,
                                   bias=T.cols[:, 2:3]).then_inc(c_made, 1)
                    act.wait_ge(b_product, k + 1)
                    act.activation(bq[:, bass.ds(k % 2 * (TT * ST), TT * ST)], prep[0][:], ACT.Copy).then_inc(b_taken, 1)

                def take_x(k):
                    act.wait_ge(x_product, k + 1)
                    half = xd[:, bass.ds(k % 2 * (TT * 256), TT * 256)].rearrange("p (t b g) -> p t b g", b=BATCH, g=ST)
                    for b in range(BATCH):
                        last = act.activation(half[:, :, b, :], prep[1][:].rearrange("p (t g) -> p t g", g=ST), ACT.Copy,
                                              scale=T.mask8[:, b:b + 1])
                    last.then_inc(xd_made, 1)

                def take_y(n):
                    for h in range(2):
                        act.wait_ge(y_made, n * 2 + h + 1)
                        for b in range(Q):
                            rows = slice(ST * b, ST * b + ST)
                            got = y_bank[h][rows, 0:P].rearrange("p (t h b q) -> p h q t b", h=GRP, b=Q, q=Q)
                            last = act.activation(ys[rows, :, :, bass.ds(n * 8 + Q * h, Q)], got[:, :, :, :, b], ACT.Copy)
                        last.then_inc(y_taken, 1)

                take_conv(0)
                take_bc(0)
                take_x(0)
                take_conv(1)
                take_y(0)
                take_bc(1)
                take_y(1)
                take_x(1)
                with act.Fori(2, 8) as n:
                    take_y(n)
                with act.Fori(1, NCH - 1) as k:
                    take_conv(k + 1)
                    take_y(k * 8)
                    take_bc(k + 1)
                    take_y(k * 8 + 1)
                    take_x(k + 1)
                    with act.Fori(2, 8) as n:
                        take_y(k * 8 + n)
                with act.Fori((NCH - 1) * 8, NCH * 8) as n:
                    take_y(n)

            @block.gpsimd
            def _(pool):
                pool.memset(state[:, 2 * Q - 1, :, :], 0.0).then_inc(zeroed, 1)

                def add_bias(k):
                    pool.wait_ge(b_taken, k + 1)
                    pool.wait_ge(c_made, k + 1)
                    pool.wait_ge(xd_made, k + 1)
                    part = bq[:, bass.ds(k % 2 * (TT * ST), TT * ST)].rearrange("p (t n) -> p t n", n=ST)
                    pool.tensor_tensor(part, part, spread(T.bb_row[:], [[0, TT], [1, ST]]), ALU.add).then_inc(b_biased, 1)

                def expand(k, q, h):
                    pool.wait_ge(b_biased, k + 1)
                    if not (isinstance(q, int) and q < 2):
                        pool.wait_ge(u_made, (q - 1) * 2)
                    b_row = bq[:, bass.ds(q % (2 * TT) * ST, ST)]
                    pool.tensor_tensor(wb[h][:].rearrange("p t (q n) -> p (t q) n", n=ST), repeat_outer(b_row, Q * Q),
                                       spread(T.mask16[:], [[1, Q * Q], [0, ST]]), ALU.mult).then_inc(wb_made, 1)
                    if not (isinstance(q, int) and q < 2):
                        pool.wait_ge(y_made, q - 1)
                    c_row = cr[:, bass.ds(q % (2 * TT) * (Q * BATCH), Q * BATCH)]
                    pool.tensor_tensor(cb[h][:].rearrange("p t b q -> p (t b) q"), repeat_inner(c_row, Q),
                                       spread(T.mask4[:], [[0, Q * BATCH], [1, Q]]), ALU.mult).then_inc(cb_made, 1)

                add_bias(0)
                expand(0, 0, 0)
                expand(0, 1, 1)
                with pool.Fori(1, 8) as n:
                    for h in range(2):
                        expand(0, n * 2 + h, h)
                with pool.Fori(1, NCH) as k:
                    add_bias(k)
                    with pool.Fori(0, 8) as n:
                        for h in range(2):
                            expand(k, k * 16 + n * 2 + h, h)

            @block.vector
            def _(dve):
                decay = spread(T.decay[:], [[0, Q], [1, ST]])
                by_b = lambda t: t.rearrange("p (b g) -> p b g", g=ST)

                def eight_steps(n):
                    for r in range(2 * Q):
                        t = n * 8 + r
                        start = isinstance(n, int) and t == 0
                        old, new = (r - 1) % (2 * Q), r
                        for half in range(GRP):
                            if start:
                                dve.wait_ge(zeroed, 1)
                            else:
                                dve.wait_ge(steps, t * 6 - 1 + half)
                            dve.tensor_tensor(by_b(scaled[:, half, :]), by_b(state[:, old, half, :]), decay,
                                              ALU.mult).then_inc(steps, 1)
                        if r % 2 == 0:
                            dve.wait_ge(u_made, n * 4 + r // 2 + 1)
                        for half in range(GRP):
                            dve.wait_ge(steps, t * 6 + 1 + half)
                            at = r % 2 * 256 + half * HALF
                            dve.tensor_tensor(summed[:, half, :], scaled[:, half, :], u_bank[r // 2][:, at:at + HALF],
                                              ALU.add).then_inc(steps, 1)
                        if r % Q == 0 and not isinstance(n, int):
                            dve.wait_ge(y_made, n * 2 + r // Q - 1)
                        for half in range(GRP):
                            dve.wait_ge(steps, t * 6 + 3 + half)
                            dve.tensor_scalar(state[:, new, half, :], summed[:, half, :], 10.0, -10.0, ALU.min, ALU.max).then_inc(steps, 1)

                eight_steps(0)
                with dve.Fori(1, NCH * 8) as n:
                    eight_steps(n)


def repeat_outer(ap, n):
    return ap.unsqueeze(1).to_broadcast([ap.shape[0], n, ap.shape[1]])


def repeat_inner(ap, n):
    return ap.unsqueeze(2).to_broadcast([ap.shape[0], ap.shape[1], n])


def project_out(nc, T):
    with ExitStack() as ctx:
        gated, made, taken, biased = (ctx.enter_context(nc.semaphore("po_" + name)) for name in ("gated", "made", "taken", "biased"))
        y = T.xt[:].rearrange("p (h q t) -> p h q t", h=GRP, q=Q)
        with nc.Block() as block:
            @block.vector
            def _(dve):
                for half in range(GRP):
                    for dq in range(Q):
                        dve.tensor_tensor(y[:, half, dq, :], y[:, half, dq, :], T.zq[:, half, dq, :], ALU.mult).then_inc(gated, 1)
                dve.wait_ge(biased, 1)
                for b in range(BATCH):
                    dve.wait_ge(made, b + 1)
                    part = T.xn[:, 4 * b:4 * b + 4, 0:D]
                    dve.tensor_tensor(part, T.bank[b % 4][:].rearrange("p (t d) -> p t d", d=D), part, ALU.add).then_inc(taken, 1)

            @block.gpsimd
            def _(pool):
                pool.tensor_tensor(T.xn[:, :, 0:D], T.xn[:, :, 0:D], spread(T.rows[:, 0, :], [[0, NT], [1, D]]), ALU.add).then_inc(biased, 1)

            @block.tensor
            def _(pe):
                for b in range(BATCH):
                    half, rows = b // Q, slice(ST * (b % Q), ST * (b % Q) + ST)
                    pe.wait_ge(gated, Q * (half + 1))
                    if b >= 4:
                        pe.wait_ge(taken, b - 3)
                    for tile in range(4):
                        for dq in range(Q):
                            last = pe.matmul(T.bank[b % 4][:, tile * D:(tile + 1) * D], y[rows, half, dq, tile * P:(tile + 1) * P],
                                             T.o_q[rows, dq, :], start=(dq == 0), stop=(dq == Q - 1))
                    last.then_inc(made, 1)


def add_normalized(nc, T):
    PARTS = 4
    with ExitStack() as ctx:
        scaled, moved, added = (ctx.enter_context(nc.semaphore("an_" + name)) for name in ("scaled", "moved", "added"))
        with nc.Block() as block:
            @block.vector
            def _(dve):
                row = lambda k: spread(T.rows[:, k, :], [[0, NT // PARTS], [1, D]])
                parts = [slice(n * NT // PARTS, (n + 1) * NT // PARTS) for n in range(PARTS)]
                for part in parts:
                    dve.tensor_tensor(T.xn[:, part, 0:D], T.xn[:, part, 0:D], row(1), ALU.mult).then_inc(scaled, 1)
                for n, part in enumerate(parts):
                    dve.wait_ge(scaled, n + 1)
                    dve.tensor_tensor(T.x[:, part, :], T.x[:, part, :], row(2), ALU.add).then_inc(moved, 1)
                for n, part in enumerate(parts):
                    dve.wait_ge(moved, n + 1)
                    dve.tensor_tensor(T.x[:, part, :], T.x[:, part, :], T.xn[:, part, 0:D], ALU.add).then_inc(added, 1)


_INS = ["L0_attn_x", "L0_attn_in_w", "L0_attn_in_b", "L0_attn_conv_w", "L0_attn_conv_b", "L0_attn_A_log", "L0_attn_B_w",
        "L0_attn_B_b", "L0_attn_C_w", "L0_attn_C_b", "L0_attn_out_w", "L0_attn_out_b", "L0_attn_ln_w", "L0_attn_ln_b",
        "L0_ffn_Wr", "L0_ffn_W1", "L0_ffn_b1", "L0_ffn_W2", "L0_ffn_b2"]


def kernel(**inputs):
    import numpy as np
    import concourse.bacc as bacc
    from concourse.bass_utils import run_bass_kernel_spmd

    nc = bacc.Bacc("TRN2", target_bir_lowering=False, num_devices=1)
    arrays, args = {}, {}
    for name in _INS:
        array = np.ascontiguousarray(inputs[name])
        arrays[name] = array
        args[name] = nc.dram_tensor(name, array.shape, mybir.dt.from_np(array.dtype), kind="ExternalInput").ap()
    out = nc.dram_tensor("out", (BATCH, L, D), F32, kind="ExternalOutput").ap()
    build(nc, args, out)
    results = run_bass_kernel_spmd(nc, [arrays], core_ids=[0])
    return results.results[0]["out"]
```

```python
from contextlib import ExitStack

import concourse.bass as bass
from concourse import mybir

F32 = mybir.dt.float32
I32 = mybir.dt.int32
U32 = mybir.dt.uint32
ALU = mybir.AluOpType
ACT = mybir.ActivationFunctionType
AX = mybir.AxisListType

P = 128
BATCH, L, D = 8, 512, 128
TOK = BATCH * L
NT = TOK // P
E, F = 8, 512
FC = F // P
ST = 32
TILES = 40
SLOTS = TILES * P
ROW = D + 1
EPS = 1e-5
WROW = FC * P + FC * P + FC + D
W2_AT, B1_AT, B2_AT = F, 2 * F, 2 * F + FC
Q = 4
CH = 64
NCH = L // CH
GRP = 2
HALF = BATCH // GRP * ST
QUADS = L // Q


def spread(ap, dims):
    return bass.AP(tensor=ap.tensor, offset=ap.offset, ap=[list(ap.ap[0])] + [list(d) for d in dims])


class Tensors:
    pass


def build(nc, a, out):
    with ExitStack() as ctx:
        def sb(name, shape, dt=F32):
            return ctx.enter_context(nc.sbuf_tensor(name, shape, dt))

        def dram(name, shape):
            return nc.dram_tensor(name, shape, F32, kind="Internal").ap()

        T = Tensors()
        T.x = sb("x", [P, NT, D])
        T.xn = sb("xn", [P, NT, ROW])
        T.xt = sb("xt", [P, TOK])
        T.tables = sb("tables", [P, E, WROW])
        T.ident = sb("ident", [P, P])
        T.before = sb("before", [P, P])
        T.ones = sb("ones", [P, P])
        T.wr = sb("wr", [P, E])
        T.tile_expert = sb("tile_expert", [P, TILES], I32)
        T.slot = sb("slot", [P, NT], U32)
        T.gate = sb("gate", [P, NT])
        T.rstd = sb("rstd", [P, NT])
        T.stat = sb("stat", [P, NT, 2])
        T.share = sb("share", [P, 2 * CH // Q * BATCH * ST])
        T.in_t = sb("in_t", [P, 2 * D])
        T.b_t = sb("b_t", [P, ST])
        T.c_rep = sb("c_rep", [P, Q, ST])
        T.o_q = sb("o_q", [P, Q, D])
        T.conv_diag = sb("conv_diag", [P, Q, P])
        T.cols = sb("cols", [P, 3 + Q])
        T.rows = sb("rows", [P, 3, D])
        T.bb_row = sb("bb_row", [P, ST])
        T.decay = sb("decay", [P, ST])
        T.mask4 = sb("mask4", [P, Q])
        T.mask8 = sb("mask8", [P, BATCH])
        T.mask16 = sb("mask16", [P, Q * Q])
        T.stack = sb("stack", [P, ST])
        T.zq = sb("zq", [P, GRP, Q, L])
        T.xa = sb("xa", [P, BATCH, L + 4])
        T.sorted = [dram(f"sorted{n}", [SLOTS, ROW]) for n in range(2)]
        T.ffn_out = [dram(f"ffn_out{n}", [TOK + SLOTS, D]) for n in range(2)]
        T.bank = [ctx.enter_context(nc.psum_tensor(f"bank{n}", [P, 512], F32)) for n in range(8)]

        setup(nc, T, a)
        for n in range(2):
            normalize(nc, T, f"n{n}_", T.x, logits=True)
            route(nc, T, f"r{n}_", T.sorted[n])
            experts(nc, T, f"e{n}_", T.sorted[n], T.ffn_out[n])
            combine(nc, T, f"c{n}_", T.ffn_out[n], out if n else None)
            if n == 0:
                normalize(nc, T, "nb_", T.x)
                project_in(nc, T)
                scan(nc, T)
                project_out(nc, T)
                normalize(nc, T, "no_", T.xn, turn=False)
                add_normalized(nc, T)
    return nc


def setup(nc, T, a):
    with ExitStack() as ctx:
        def sem(name):
            return ctx.enter_context(nc.semaphore("s_" + name))

        def sb(name, shape, dt=F32):
            return ctx.enter_context(nc.sbuf_tensor("s_" + name, shape, dt))

        x_in, w_in, tables_in, small_in, pads_out = map(sem, ("x_in", "w_in", "tables_in", "small_in", "pads_out"))
        pool_made, dve_made, pe_made, act_made = map(sem, ("pool_made", "dve_made", "pe_made", "act_made"))
        in_w = sb("in_w", [P, 2, D])
        bc_w = sb("bc_w", [2 * ST, D])
        out_w = sb("out_w", [P, D])
        b1 = sb("b1", [E * FC, P])
        taps = sb("taps", [P, Q])
        a_log = sb("a_log", [P, ST])
        a_t = sb("a_t", [P, ST])
        fill = T.share[:, 0:TILES * ROW].rearrange("p (i r) -> p i r", r=ROW)

        with nc.Block() as block:
            @block.sync
            def _(sp):
                sp.dma_start(T.x[:], a["L0_attn_x"].rearrange("b (q p) d -> p (b q) d", p=P)).then_inc(x_in, 16)
                sp.dma_start(T.wr[:], a["L0_ffn_Wr"]).then_inc(w_in, 16)
                sp.dma_start(in_w[:], a["L0_attn_in_w"].rearrange("(h p) c -> p h c", p=P)).then_inc(w_in, 16)
                sp.dma_start(bc_w[0:ST, :], a["L0_attn_B_w"]).then_inc(w_in, 16)
                sp.dma_start(bc_w[ST:2 * ST, :], a["L0_attn_C_w"]).then_inc(w_in, 16)
                sp.dma_start(out_w[:], a["L0_attn_out_w"]).then_inc(w_in, 16)
                sp.dma_start(b1[:], a["L0_ffn_b1"].rearrange("e (c p) -> (e c) p", p=P)).then_inc(w_in, 16)
                sp.dma_start(taps[:], a["L0_attn_conv_w"].rearrange("c o k -> c (o k)")).then_inc(w_in, 16)
                sp.dma_start(a_log[:], a["L0_attn_A_log"]).then_inc(w_in, 16)
                sp.dma_start(T.tables[:, :, 0:F], a["L0_ffn_W1"].rearrange("e d f -> d e f")).then_inc(tables_in, 16)
                for e in range(E):
                    sp.dma_start(T.tables[:, e, W2_AT:W2_AT + F].rearrange("p (c d) -> p c d", d=D),
                                 a["L0_ffn_W2"][e].rearrange("(c p) d -> p c d", p=P)).then_inc(tables_in, 16)
                sp.wait_ge(pool_made, 4)
                for n in range(2):
                    sp.dma_start(T.sorted[n].rearrange("(i p) r -> p i r", p=P), fill).then_inc(pads_out, 16)
                sp.wait_ge(pads_out, 32)
                sp.wait_ge(tables_in, 16 * (1 + E))
                sp.wait_ge(x_in, 16)

            @block.scalar
            def _(act):
                for k, name in enumerate(("L0_attn_out_b", "L0_attn_ln_w", "L0_attn_ln_b")):
                    act.dma_start(T.rows[:, k, :], bass.AP(tensor=a[name].tensor, offset=0, ap=[[0, P], [1, D]])).then_inc(small_in, 16)
                act.dma_start(T.bb_row[:], bass.AP(tensor=a["L0_attn_B_b"].tensor, offset=0, ap=[[0, P], [1, ST]])).then_inc(small_in, 16)
                act.dma_start(T.tables[:, :, B2_AT:B2_AT + D],
                              bass.AP(tensor=a["L0_ffn_b2"].tensor, offset=0, ap=[[0, P], [D, E], [1, D]])).then_inc(small_in, 16)
                column = lambda name, at, step=1, n=P: bass.AP(tensor=a[name].tensor, offset=at, ap=[[step, n], [1, 1]])
                act.dma_start(T.cols[:, 0:1], column("L0_attn_in_b", 0)).then_inc(small_in, 16)
                act.dma_start(T.cols[:, 1:2], column("L0_attn_conv_b", 0)).then_inc(small_in, 16)
                for b in range(Q):
                    rows = slice(ST * b, ST * b + ST)
                    act.dma_start(T.cols[rows, 2:3], column("L0_attn_C_b", 0, n=ST)).then_inc(small_in, 16)
                    for dq in range(Q):
                        act.dma_start(T.cols[rows, 3 + dq:4 + dq], column("L0_attn_in_b", D + dq * ST, n=ST)).then_inc(small_in, 16)
                act.wait_ge(dve_made, 2)
                act.activation(T.decay[:], a_t[:], ACT.Exp).then_inc(act_made, 1)
                act.wait_ge(small_in, 16 * (7 + Q * (1 + Q)))

            @block.gpsimd
            def _(pool):
                pool.memset(T.ones[:], 1.0).then_inc(pool_made, 1)
                pool.memset(fill[:, :, 0:D], 0.0).then_inc(pool_made, 1)
                pool.iota(fill.bitcast(I32)[:, :, D:ROW], pattern=[[P, TILES]], base=TOK, channel_multiplier=1).then_inc(pool_made, 1)
                pool.iota(T.xn[:].bitcast(I32)[:, :, D:ROW], pattern=[[P, NT]], base=0, channel_multiplier=1).then_inc(pool_made, 1)
                pool.wait_ge(pool_made, 1)
                pool.affine_select(out=T.ident[:], in_=T.ones[:], compare_op=ALU.is_equal, fill=0.0,
                                   base=0, pattern=[[-1, P]], channel_multiplier=1).then_inc(pool_made, 1)
                pool.affine_select(out=T.before[:], in_=T.ones[:], compare_op=ALU.is_gt, fill=0.0,
                                   base=0, pattern=[[1, P]], channel_multiplier=-1).then_inc(pool_made, 1)
                pool.memset(T.xa[:], 0.0).then_inc(pool_made, 1)

            @block.vector
            def _(dve):
                dve.wait_ge(w_in, 16 * 8)
                dve.tensor_scalar(a_log[:], a_log[:], -5.0, 2.0, ALU.max, ALU.min).then_inc(dve_made, 1)
                dve.wait_ge(dve_made, 1)
                dve.transpose(a_t[:], a_log[:]).then_inc(dve_made, 1)
                dve.wait_ge(pool_made, 7)
                ident = T.ident[:]
                dve.tensor_reduce(T.mask4[:], ident.rearrange("p (i k) -> p i k", i=Q), AX.X, ALU.add).then_inc(dve_made, 1)
                dve.tensor_reduce(T.mask16[:], ident.rearrange("p (i k) -> p i k", i=Q * Q), AX.X, ALU.add).then_inc(dve_made, 1)
                dve.tensor_reduce(T.mask8[:], ident.rearrange("p (k i) -> p i k", i=BATCH), AX.X, ALU.add).then_inc(dve_made, 1)
                dve.tensor_reduce(T.stack[:], ident.rearrange("p (k i) -> p i k", i=ST), AX.X, ALU.add).then_inc(dve_made, 1)
                for k in range(Q):
                    dve.tensor_scalar(T.conv_diag[:, k, :], ident, taps[:, k:k + 1], None, ALU.mult).then_inc(dve_made, 1)
                dve.wait_ge(pe_made, 1)
                dve.tensor_copy(T.in_t[:], T.bank[0][:, 0:2 * D]).then_inc(dve_made, 1)
                dve.tensor_copy(T.b_t[:], T.bank[1][:, 0:ST]).then_inc(dve_made, 1)
                dve.tensor_copy(T.c_rep[:], spread(T.bank[1][:, ST:2 * ST], [[0, Q], [1, ST]])).then_inc(dve_made, 1)
                dve.tensor_copy(T.tables[:, :, B1_AT:B1_AT + FC],
                                T.bank[2][:, 0:E * FC].rearrange("p (e c) -> p e c", c=FC)).then_inc(dve_made, 1)
                dve.tensor_copy(T.o_q[:], T.bank[3][:, 0:Q * D].rearrange("p (q d) -> p q d", d=D)).then_inc(dve_made, 1)
                dve.wait_ge(act_made, 1)
                dve.tensor_scalar(T.decay[:], T.decay[:], -1.0, None, ALU.mult).then_inc(dve_made, 1)

            @block.tensor
            def _(pe):
                pe.wait_ge(w_in, 16 * 8)
                pe.wait_ge(pool_made, 7)
                for h in range(2):
                    pe.transpose(T.bank[0][:, h * D:(h + 1) * D], in_w[:, h, :], T.ident[:])
                pe.transpose(T.bank[1][:, 0:2 * ST], bc_w[:], T.ident[0:2 * ST, 0:2 * ST])
                pe.transpose(T.bank[2][:, 0:E * FC], b1[:], T.ident[0:E * FC, 0:E * FC])
                for b in range(Q):
                    for dq in range(Q):
                        last = pe.matmul(T.bank[3][ST * b:ST * b + ST, dq * D:(dq + 1) * D],
                                         out_w[:, dq * ST:(dq + 1) * ST], T.ident[:], start=True, stop=True)
                last.then_inc(pe_made, 1)


def normalize(nc, T, tag, src, turn=True, logits=False):
    with ExitStack() as ctx:
        def sem(name):
            return ctx.enter_context(nc.semaphore(tag + name))

        def sb(name, shape, dt=F32):
            return ctx.enter_context(nc.sbuf_tensor(tag + name, shape, dt))

        stats_made, aggregated, chain, root_made, normed, transposed, xt_made = map(
            sem, ("stats_made", "aggregated", "chain", "root_made", "normed", "transposed", "xt_made"))
        raw = sb("raw", [P, NT, 6])
        var = sb("var", [P, NT])
        tmp = sb("tmp", [P, NT])
        with nc.Block() as block:
            @block.vector
            def _(dve):
                for j in range(NT):
                    dve.bn_stats(raw[:, j, :], src[:, j, 0:D]).then_inc(stats_made, 1)
                for j in range(NT):
                    dve.wait_ge(stats_made, j + 1)
                    dve.bn_aggr(T.stat[:, j, :], raw[:, j, :]).then_inc(aggregated, 1)
                dve.wait_ge(aggregated, NT)
                dve.tensor_scalar(var[:], T.stat[:, :, 1], EPS, None, ALU.add).then_inc(chain, 1)
                dve.wait_ge(root_made, 1)
                dve.reciprocal(T.rstd[:], tmp[:]).then_inc(chain, 1)
                dve.wait_ge(chain, 2)
                dve.tensor_tensor(tmp[:], T.rstd[:], T.rstd[:], ALU.mult).then_inc(chain, 1)
                dve.wait_ge(chain, 3)
                dve.tensor_tensor(tmp[:], tmp[:], var[:], ALU.mult).then_inc(chain, 1)
                dve.wait_ge(chain, 4)
                dve.tensor_scalar(tmp[:], tmp[:], -0.5, 1.5, ALU.mult, ALU.add).then_inc(chain, 1)
                dve.wait_ge(chain, 5)
                dve.tensor_tensor(T.rstd[:], T.rstd[:], tmp[:], ALU.mult).then_inc(chain, 1)
                dve.wait_ge(chain, 6)
                for j in range(NT):
                    dve.tensor_scalar(T.xn[:, j, 0:D], src[:, j, 0:D], T.stat[:, j, 0:1], T.rstd[:, j:j + 1],
                                      ALU.subtract, ALU.mult).then_inc(normed, 1)

            @block.scalar
            def _(act):
                act.wait_ge(chain, 1)
                act.activation(tmp[:], var[:], ACT.Sqrt).then_inc(root_made, 1)
                for g in range(NT // 4 if turn else 0):
                    act.wait_ge(transposed, g + 1)
                    act.activation(T.xt[:, g * 512:(g + 1) * 512], T.bank[g % 2][:], ACT.Copy).then_inc(xt_made, 1)

            @block.tensor
            def _(pe):
                for g in range(NT // 4 + 1 if turn else 0):
                    if g < NT // 4:
                        if g >= 2:
                            pe.wait_ge(xt_made, g - 1)
                        for j in range(4 * g, 4 * g + 4):
                            pe.wait_ge(normed, j + 1)
                            last = pe.transpose(T.bank[g % 2][:, (j % 4) * P:(j % 4 + 1) * P], T.xn[:, j, 0:D], T.ident[:])
                        last.then_inc(transposed, 1)
                    if g >= 1 and logits:
                        pe.wait_ge(xt_made, g)
                        for j in range(4 * g - 4, 4 * g):
                            pe.matmul(T.bank[2][:, j * E:(j + 1) * E], T.xt[:, j * P:(j + 1) * P], T.wr[:],
                                      start=True, stop=True)


def route(nc, T, tag, sorted_rows):
    with ExitStack() as ctx:
        def sem(name):
            return ctx.enter_context(nc.semaphore(tag + name))

        def sb(name, shape, dt=F32):
            return ctx.enter_context(nc.sbuf_tensor(tag + name, shape, dt))

        chain, exps_made, counted, const_made, scattered = map(
            sem, ("chain", "exps_made", "counted", "const_made", "scattered"))
        logits = sb("logits", [P, E, NT])
        exps = sb("exps", [P, E, NT])
        pick = sb("pick", [P, E, NT])
        place = sb("place", [P, E, NT])
        upto = sb("upto", [P, E, NT])
        carry = sb("carry", [P, E, NT])
        best = sb("best", [P, NT])
        total = sb("total", [P, NT])
        rank_e = sb("rank_e", [P, E])
        count = sb("count", [P, E], I32)
        tiles = sb("tiles", [P, E])
        ends = sb("ends", [P, E])
        base = sb("base", [P, E])
        tile_no = sb("tile_no", [P, TILES])
        past = sb("past", [P, TILES, E])
        tile_e = sb("tile_e", [P, TILES])

        by_tile = lambda t: t[:].rearrange("p e j -> p j e")
        over_e = lambda t: spread(t[:], [[0, E], [1, NT]])
        over_j = lambda t: spread(t[:], [[1, E], [0, NT]])

        with nc.Block() as block:
            @block.gpsimd
            def _(pool):
                pool.memset(carry[:], 1.0).then_inc(const_made, 1)
                pool.iota(rank_e[:], pattern=[[-1, E]], base=E, channel_multiplier=0,
                          allow_small_or_imprecise_dtypes=True).then_inc(const_made, 1)
                pool.iota(tile_no[:], pattern=[[1, TILES]], base=0, channel_multiplier=0,
                          allow_small_or_imprecise_dtypes=True).then_inc(const_made, 1)
                pool.wait_ge(const_made, 3)
                pool.memset(carry[:, :, 0:1], 0.0).then_inc(const_made, 1)
                pool.wait_ge(chain, 25)
                for j in range(NT):
                    pool.indirect_dma_start(sorted_rows, bass.IndirectOffsetOnAxis(ap=T.slot[:, j:j + 1], axis=0),
                                            T.xn[:, j, :], None).then_inc(scattered, 16)
                pool.wait_ge(scattered, 16 * NT)

            @block.scalar
            def _(act):
                act.wait_ge(chain, 3)
                act.activation(exps[:], logits[:], ACT.Exp).then_inc(exps_made, 1)

            @block.tensor
            def _(pe):
                pe.wait_ge(chain, 7)
                pe.matmul(T.bank[0][:, 0:E * NT], T.before[:], pick[:].rearrange("p e j -> p (e j)"), start=True, stop=True)
                pe.matmul(T.bank[1][:, 0:E * NT], T.ones[:], pick[:].rearrange("p e j -> p (e j)"),
                          start=True, stop=True).then_inc(counted, 1)

            @block.vector
            def _(dve):
                done = [0]

                def then(instruction):
                    done[0] += 1
                    instruction.then_inc(chain, 1)
                    dve.wait_ge(chain, done[0])

                then(dve.tensor_copy(logits[:], T.bank[2][:, 0:E * NT].rearrange("p (j e) -> p e j", e=E)))
                then(dve.tensor_reduce(best[:], by_tile(logits), AX.X, ALU.max))
                then(dve.tensor_tensor(logits[:], logits[:], over_e(best), ALU.subtract))
                then(dve.tensor_scalar(pick[:], logits[:], 0.0, None, ALU.is_equal))
                dve.wait_ge(const_made, 4)
                then(dve.tensor_tensor(pick[:], pick[:], over_j(rank_e), ALU.mult))
                then(dve.tensor_reduce(best[:], by_tile(pick), AX.X, ALU.max))
                then(dve.tensor_tensor(pick[:], pick[:], over_e(best), ALU.is_equal))
                dve.wait_ge(exps_made, 1)
                then(dve.tensor_reduce(total[:], by_tile(exps), AX.X, ALU.add))
                then(dve.reciprocal(T.gate[:], total[:]))
                then(dve.tensor_scalar(T.gate[:], T.gate[:], 0.5, None, ALU.mult))
                dve.wait_ge(counted, 1)
                flat = lambda t: t[:].rearrange("p e j -> p (e j)")
                then(dve.tensor_tensor_scan(flat(upto), flat(carry), T.bank[1][:, 0:E * NT], 0.0, ALU.mult, ALU.add))
                then(dve.tensor_tensor(flat(place), flat(upto), T.bank[1][:, 0:E * NT], ALU.subtract))
                then(dve.tensor_tensor(flat(place), flat(place), T.bank[0][:, 0:E * NT], ALU.add))
                then(dve.tensor_scalar(count[:], upto[:, :, NT - 1], float(P - 1), None, ALU.add))
                then(dve.tensor_scalar(count[:], count[:], P.bit_length() - 1, None, ALU.arith_shift_right))
                then(dve.tensor_copy(tiles[:], count[:]))
                then(dve.tensor_tensor_scan(ends[:], T.ones[:, 0:E], tiles[:], 0.0, ALU.mult, ALU.add))
                then(dve.tensor_tensor(base[:], ends[:], tiles[:], ALU.subtract))
                then(dve.tensor_scalar(base[:], base[:], float(P), None, ALU.mult))
                then(dve.tensor_tensor(place[:], place[:], over_j(base), ALU.add))
                then(dve.tensor_tensor(place[:], place[:], pick[:], ALU.mult))
                then(dve.tensor_tensor(past[:], spread(tile_no[:], [[1, TILES], [0, E]]),
                                       spread(ends[:], [[0, TILES], [1, E]]), ALU.is_ge))
                then(dve.tensor_reduce(best[:], by_tile(place), AX.X, ALU.add))
                then(dve.tensor_reduce(tile_e[:], past[:], AX.X, ALU.add))
                then(dve.tensor_copy(T.slot[:], best[:]))
                then(dve.tensor_scalar(T.tile_expert[:], tile_e[:], float(E - 1), None, ALU.min))


def experts(nc, T, tag, sorted_rows, ffn_out):
    RING = 8
    STAGES = TILES // RING
    AHEAD = 4
    with ExitStack() as ctx:
        def sem(name):
            return ctx.enter_context(nc.semaphore(tag + name))

        def sb(name, shape, dt=F32):
            return ctx.enter_context(nc.sbuf_tensor(tag + name, shape, dt))

        loaded = [sem(f"loaded{r}") for r in range(RING)]
        stored = [sem(f"stored{r}") for r in range(RING)]
        turned, x_made, w_made, up_made, h_made, down_made, out_made = map(
            sem, ("turned", "x_made", "w_made", "up_made", "h_made", "down_made", "out_made"))
        rows = [sb(f"rows{r}", [P, ROW]) for r in range(RING)]
        outs = [sb(f"outs{r}", [P, D]) for r in range(RING)]
        xt = [sb(f"xt{r}", [P, P]) for r in range(AHEAD)]
        weights = [sb(f"weights{r}", [P, WROW]) for r in range(AHEAD)]
        hidden = [sb(f"hidden{r}", [P, FC, P]) for r in range(2)]
        turn, up, down = T.bank[0:2], T.bank[2:4], T.bank[4:6]

        def stages(eng, stage):
            stage(0, True, False)
            with eng.Fori(1, STAGES - 1) as s:
                stage(s, False, False)
            stage(STAGES - 1, False, True)

        with nc.Block() as block:
            @block.sync
            def _(sp):
                for r in range(RING):
                    sp.dma_start(rows[r][:], sorted_rows[r * P:(r + 1) * P, :]).then_inc(loaded[r], 16)
                with sp.Fori(1, STAGES) as s:
                    for r in range(RING):
                        sp.wait_ge(stored[r], s * 16)
                        sp.dma_start(rows[r][:], sorted_rows[bass.ds((s * RING + r) * P, P), :]).then_inc(loaded[r], 16)

            @block.tensor
            def _(pe):
                def turn_in(s, r, i, early):
                    pe.wait_ge(loaded[r], (s + 1) * 16)
                    if not early:
                        pe.wait_ge(x_made, i - 1)
                    pe.transpose(turn[r % 2][:, 0:P], rows[r][:, 0:D], T.ident[:]).then_inc(turned, 1)

                def go_up(i, r, early):
                    pe.wait_ge(x_made, i + 1)
                    pe.wait_ge(w_made, i + 1)
                    if not early:
                        pe.wait_ge(h_made, i - 1)
                    for c in range(FC):
                        last = pe.matmul(up[r % 2][:, c * P:(c + 1) * P], weights[r % AHEAD][:, c * P:(c + 1) * P],
                                         xt[r % AHEAD][:], start=True, stop=True)
                    last.then_inc(up_made, 1)

                def go_down(i, r, early):
                    pe.wait_ge(h_made, i + 1)
                    if not early:
                        pe.wait_ge(out_made, i - 1)
                    for c in range(FC):
                        last = pe.matmul(down[r % 2][:, 0:D], hidden[r % 2][:, c, :],
                                         weights[r % AHEAD][:, W2_AT + c * D:W2_AT + (c + 1) * D],
                                         start=(c == 0), stop=(c == FC - 1))
                    last.then_inc(down_made, 1)

                def stage(s, first, last):
                    for r in range(RING):
                        i = s * RING + r
                        if not (last and r >= RING - 2):
                            turn_in(s + (r + 2) // RING, (r + 2) % RING, i + 2, False)
                        go_up(i, r, first and r < 2)
                        if not (first and r == 0):
                            go_down(i - 1, (r - 1) % RING, first and r < 3)

                turn_in(0, 0, 0, True)
                turn_in(0, 1, 1, True)
                stages(pe, stage)
                go_down(TILES - 1, RING - 1, False)

            @block.scalar
            def _(act):
                def stage(s, first, last):
                    for r in range(RING):
                        act.wait_ge(up_made, s * RING + r + 1)
                        for c in range(FC):
                            made = act.activation(hidden[r % 2][:, c, :], up[r % 2][:, c * P:(c + 1) * P], ACT.Gelu,
                                                  bias=weights[r % AHEAD][:, B1_AT + c:B1_AT + c + 1])
                        made.then_inc(h_made, 1)

                stages(act, stage)

            @block.vector
            def _(dve):
                def take_weights(i, r, early):
                    e = dve.value_load(T.tile_expert[0:1, bass.ds(i, 1)], min_val=0, max_val=E - 1)
                    if not early:
                        dve.wait_ge(down_made, i - AHEAD + 1)
                        dve.wait_ge(out_made, i - AHEAD + 1)
                    flat = T.tables[:].rearrange("p e w -> p (e w)")
                    dve.tensor_copy(weights[r % AHEAD][:], flat[:, bass.ds(e * WROW, WROW)]).then_inc(w_made, 1)

                def take_x(i, r):
                    dve.wait_ge(turned, i + 1)
                    dve.tensor_copy(xt[r % AHEAD][:], turn[r % 2][:, 0:P]).then_inc(x_made, 1)

                def give_out(i, r):
                    dve.wait_ge(down_made, i + 1)
                    dve.tensor_tensor(outs[r][:], down[r % 2][:, 0:D], weights[r % AHEAD][:, B2_AT:B2_AT + D],
                                      ALU.add).then_inc(out_made, 1)

                def stage(s, first, last):
                    for r in range(RING):
                        i = s * RING + r
                        if not (last and r >= RING - 2):
                            take_x(i + 2, (r + 2) % RING)
                            take_weights(i + 2, (r + 2) % RING, first and r < 2)
                        if not (first and r == 0):
                            give_out(i - 1, (r - 1) % RING)

                for i in range(2):
                    take_x(i, i)
                    take_weights(i, i, True)
                stages(dve, stage)
                give_out(TILES - 1, RING - 1)

            @block.gpsimd
            def _(pool):
                for s in range(STAGES):
                    for r in range(RING):
                        pool.wait_ge(out_made, s * RING + r + 1)
                        pool.indirect_dma_start(ffn_out, bass.IndirectOffsetOnAxis(ap=rows[r][:, D:ROW].bitcast(U32), axis=0),
                                                outs[r][:], None).then_inc(stored[r], 16)
                for r in range(RING):
                    pool.wait_ge(stored[r], 16 * STAGES)


def combine(nc, T, tag, ffn_out, out):
    PARTS = 4
    with ExitStack() as ctx:
        def sem(name):
            return ctx.enter_context(nc.semaphore(tag + name))

        loaded = [sem(f"loaded{n}") for n in range(PARTS)]
        added, stored = sem("added"), sem("stored")
        got = T.share[:, 0:NT * D].rearrange("p (j d) -> p j d", d=D)
        with nc.Block() as block:
            @block.sync
            def _(sp):
                rows = ffn_out[0:TOK, :].rearrange("(j p) d -> p j d", p=P)
                for n in range(PARTS):
                    part = slice(n * NT // PARTS, (n + 1) * NT // PARTS)
                    sp.dma_start(got[:, part, :], rows[:, part, :]).then_inc(loaded[n], 16)
                if out is not None:
                    to = out.rearrange("b (q p) d -> p (b q) d", p=P)
                    for n in range(PARTS):
                        part = slice(n * NT // PARTS, (n + 1) * NT // PARTS)
                        sp.wait_ge(added, (n + 1) * NT // PARTS)
                        sp.dma_start(to[:, part, :], T.x[:, part, :]).then_inc(stored, 16)
                    sp.wait_ge(stored, 16 * PARTS)

            @block.vector
            def _(dve):
                for j in range(NT):
                    if j % (NT // PARTS) == 0:
                        dve.wait_ge(loaded[j * PARTS // NT], 16)
                    dve.scalar_tensor_tensor(T.x[:, j, :], got[:, j, :], T.gate[:, j:j + 1], T.x[:, j, :],
                                             ALU.mult, ALU.add).then_inc(added, 1)


def project_in(nc, T):
    with ExitStack() as ctx:
        made, taken = ctx.enter_context(nc.semaphore("pi_made")), ctx.enter_context(nc.semaphore("pi_taken"))
        with nc.Block() as block:
            @block.tensor
            def _(pe):
                for n in range(2 * BATCH):
                    bank = T.bank[n % 4]
                    if n >= 4:
                        pe.wait_ge(taken, n - 3)
                    if n < BATCH:
                        last = pe.matmul(bank[:], T.in_t[:, 0:D], T.xt[:, n * L:(n + 1) * L], start=True, stop=True)
                    else:
                        half, dq = (n - BATCH) // Q, (n - BATCH) % Q
                        for b in range(Q):
                            at = (half * Q + b) * L
                            last = pe.matmul(bank[ST * b:ST * b + ST, :], T.in_t[:, D + dq * ST:D + (dq + 1) * ST],
                                             T.xt[:, at:at + L], start=True, stop=True)
                    last.then_inc(made, 1)

            @block.scalar
            def _(act):
                for n in range(2 * BATCH):
                    act.wait_ge(made, n + 1)
                    if n < BATCH:
                        act.activation(T.xa[:, n, 2:2 + L], T.bank[n % 4][:], ACT.Identity,
                                       bias=T.cols[:, 0:1]).then_inc(taken, 1)
                    else:
                        half, dq = (n - BATCH) // Q, (n - BATCH) % Q
                        act.activation(T.zq[:, half, dq, :], T.bank[n % 4][:], ACT.Silu,
                                       bias=T.cols[:, 3 + dq:4 + dq]).then_inc(taken, 1)


def scan(nc, T):
    with ExitStack() as ctx:
        def sem(name):
            return ctx.enter_context(nc.semaphore("sc_" + name))

        def sb(name, shape, dt=F32):
            return ctx.enter_context(nc.sbuf_tensor("sc_" + name, shape, dt))

        conv_made, xc_made, xr_made, xq_made, c_product, c_made, b_product, b_taken, x_product, xd_made = map(
            sem, ("conv_made", "xc_made", "xr_made", "xq_made", "c_product", "c_made", "b_product", "b_taken", "x_product", "xd_made"))
        b_biased, wb_made, cb_made, u_made, y_made, y_taken = map(
            sem, ("b_biased", "wb_made", "cb_made", "u_made", "y_made", "y_taken"))
        steps = sem("steps")
        zeroed = sem("zeroed")

        TT = CH // Q
        xc = sb("xc", [P, BATCH, CH])
        xr = sb("xr", [P, CH, Q, BATCH])
        xq = sb("xq", [P, CH, Q, BATCH])
        cr = sb("cr", [P, 2 * CH * BATCH])
        bq = sb("bq", [P, 2 * TT * ST])
        xd = T.share
        wb = [sb(f"wb{h}", [P, Q, P]) for h in range(2)]
        cb = [sb(f"cb{h}", [P, Q, GRP, P]) for h in range(2)]
        state = sb("state", [P, 2 * Q, GRP, HALF])
        scaled = sb("scaled", [P, GRP, HALF])
        summed = sb("summed", [P, GRP, HALF])
        ys = T.xt[:].rearrange("p (h m) -> p h m", h=GRP)
        u_bank, y_bank, prep = T.bank[0:4], T.bank[4:6], T.bank[6:8]

        with nc.Block() as block:
            @block.tensor
            def _(pe):
                def convolve(k):
                    if not (isinstance(k, int) and k == 0):
                        pe.wait_ge(b_taken, k)
                    for tap in range(4):
                        last = pe.matmul(prep[0][:], T.conv_diag[:, tap, :], T.xa[:, :, bass.ds(k * CH + tap, CH)],
                                         start=(tap == 0), stop=(tap == 3))
                    last.then_inc(conv_made, 1)

                def project(k):
                    pe.wait_ge(xc_made, k + 1)
                    if not (isinstance(k, int) and k == 0):
                        pe.wait_ge(xd_made, k)
                    pe.matmul(prep[1][:], T.c_rep[:].rearrange("p q n -> p (q n)"),
                              xc[:].rearrange("p b t -> p t b"), start=True, stop=True).then_inc(c_product, 1)
                    pe.wait_ge(xr_made, k + 1)
                    for tt in range(TT):
                        last = pe.matmul(prep[0][:, tt * ST:(tt + 1) * ST],
                                         xr[:, Q * tt:Q * tt + Q, :, :].rearrange("p t q b -> p (t q b)"), T.b_t[:],
                                         start=True, stop=True)
                    last.then_inc(b_product, 1)

                def regroup(k):
                    pe.wait_ge(xq_made, k + 1)
                    pe.wait_ge(c_made, k + 1)
                    for tt in range(TT):
                        last = pe.matmul(prep[1][:, tt * ST:(tt + 1) * ST],
                                         xq[:, Q * tt:Q * tt + Q, :, :].rearrange("p t q b -> p (t q b)"), T.stack[:],
                                         start=True, stop=True)
                    last.then_inc(x_product, 1)

                def outer(q, h):
                    pe.wait_ge(wb_made, q + 1)
                    for m in range(2):
                        if not (isinstance(q, int) and q < 2):
                            pe.wait_ge(steps, (q * 2 + m - 4) * 12 + 10)
                        for i in range(2):
                            last = pe.matmul(u_bank[2 * h + m][:, i * 256:(i + 1) * 256], wb[h][:, 2 * m + i, :],
                                             xd[:, bass.ds(q % (2 * TT) * 256, 256)], start=True, stop=True)
                        last.then_inc(u_made, 1)

                def contract(q, h):
                    pe.wait_ge(cb_made, q + 1)
                    if h == 0 and not (isinstance(q, int) and q == 0):
                        pe.wait_ge(y_taken, q // 2)
                    pe.wait_ge(steps, (q + 1) * 24)
                    for i in range(Q):
                        for half in range(GRP):
                            last = pe.matmul(y_bank[half][:, 0:HALF], cb[h][:, i, half, :], state[:, Q * h + i, half, :],
                                             start=(h == 0 and i == 0), stop=(h == 1 and i == Q - 1))
                    last.then_inc(y_made, 1)

                def eight_steps(n):
                    for h in range(2):
                        outer(n * 2 + h + 1, (h + 1) % 2)
                        if not (isinstance(n, int) and n * 2 + h == 0):
                            contract(n * 2 + h - 1, (h + 1) % 2)

                convolve(0)
                project(0)
                regroup(0)
                outer(0, 0)
                convolve(1)
                eight_steps(0)
                project(1)
                eight_steps(1)
                regroup(1)
                with pe.Fori(2, 8) as n:
                    eight_steps(n)
                with pe.Fori(1, NCH - 1) as k:
                    convolve(k + 1)
                    eight_steps(k * 8)
                    project(k + 1)
                    eight_steps(k * 8 + 1)
                    regroup(k + 1)
                    with pe.Fori(2, 8) as n:
                        eight_steps(k * 8 + n)
                with pe.Fori((NCH - 1) * 8, NCH * 8 - 1) as n:
                    eight_steps(n)
                outer(QUADS - 1, 1)
                contract(QUADS - 3, 1)
                contract(QUADS - 2, 0)
                contract(QUADS - 1, 1)

            @block.scalar
            def _(act):
                def take_conv(k):
                    act.wait_ge(conv_made, k + 1)
                    act.activation(xc[:].rearrange("p b t -> p (b t)"), prep[0][:], ACT.Silu, bias=T.cols[:, 1:2]).then_inc(xc_made, 1)
                    act.wait_ge(xc_made, k + 1)
                    act.activation(xr[:], spread(xc[:, 0, 0:1], [[1, CH], [0, Q], [CH, BATCH]]), ACT.Copy).then_inc(xr_made, 1)
                    for dq in range(Q):
                        last = act.activation(xq[:, :, dq, :], xc[:].rearrange("p b t -> p t b"), ACT.Copy,
                                              scale=T.mask4[:, dq:dq + 1])
                    last.then_inc(xq_made, 1)

                def take_bc(k):
                    act.wait_ge(c_product, k + 1)
                    act.activation(cr[:, bass.ds(k % 2 * (CH * BATCH), CH * BATCH)], prep[1][:], ACT.Identity,
                                   bias=T.cols[:, 2:3]).then_inc(c_made, 1)
                    act.wait_ge(b_product, k + 1)
                    act.activation(bq[:, bass.ds(k % 2 * (TT * ST), TT * ST)], prep[0][:], ACT.Copy).then_inc(b_taken, 1)

                def take_x(k):
                    act.wait_ge(x_product, k + 1)
                    half = xd[:, bass.ds(k % 2 * (TT * 256), TT * 256)].rearrange("p (t b g) -> p t b g", b=BATCH, g=ST)
                    for b in range(BATCH):
                        last = act.activation(half[:, :, b, :], prep[1][:].rearrange("p (t g) -> p t g", g=ST), ACT.Copy,
                                              scale=T.mask8[:, b:b + 1])
                    last.then_inc(xd_made, 1)

                def take_y(n):
                    act.wait_ge(y_made, n * 2 + 2)
                    for b in range(Q):
                        rows = slice(ST * b, ST * b + ST)
                        for half in range(GRP):
                            last = act.activation(ys[rows, half, bass.ds(n * ST, ST)], y_bank[half][rows, ST * b:ST * b + ST], ACT.Copy)
                    last.then_inc(y_taken, 1)

                take_conv(0)
                take_bc(0)
                take_x(0)
                take_conv(1)
                take_y(0)
                take_bc(1)
                take_y(1)
                take_x(1)
                with act.Fori(2, 8) as n:
                    take_y(n)
                with act.Fori(1, NCH - 1) as k:
                    take_conv(k + 1)
                    take_y(k * 8)
                    take_bc(k + 1)
                    take_y(k * 8 + 1)
                    take_x(k + 1)
                    with act.Fori(2, 8) as n:
                        take_y(k * 8 + n)
                with act.Fori((NCH - 1) * 8, NCH * 8) as n:
                    take_y(n)

            @block.gpsimd
            def _(pool):
                pool.memset(state[:, 2 * Q - 1, :, :], 0.0).then_inc(zeroed, 1)
                for h in range(2):
                    pool.memset(cb[h][:], 0.0).then_inc(zeroed, 1)
                pool.wait_ge(zeroed, 3)

                def add_bias(k):
                    pool.wait_ge(b_taken, k + 1)
                    pool.wait_ge(c_made, k + 1)
                    pool.wait_ge(xd_made, k + 1)
                    part = bq[:, bass.ds(k % 2 * (TT * ST), TT * ST)].rearrange("p (t n) -> p t n", n=ST)
                    pool.tensor_tensor(part, part, spread(T.bb_row[:], [[0, TT], [1, ST]]), ALU.add).then_inc(b_biased, 1)
                    pool.wait_ge(b_biased, k + 1)

                def expand_b(q, h):
                    if not (isinstance(q, int) and q < 2):
                        pool.wait_ge(u_made, (q - 1) * 2)
                    b_row = bq[:, bass.ds(q % (2 * TT) * ST, ST)]
                    pool.tensor_tensor(wb[h][:].rearrange("p t (q n) -> p (t q) n", n=ST), repeat_outer(b_row, Q * Q),
                                       spread(T.mask16[:], [[1, Q * Q], [0, ST]]), ALU.mult).then_inc(wb_made, 1)

                def expand_c(q, h):
                    if not (isinstance(q, int) and q < 2):
                        pool.wait_ge(y_made, q - 1)
                    c_row = cr[:, bass.ds(q % (2 * TT) * (Q * BATCH), Q * BATCH)]
                    at = Q * Q * h
                    pool.tensor_tensor(spread(cb[h][:, 0, 0, at:at + 1], [[GRP * P + Q, Q], [ST, BATCH], [1, Q]]),
                                       c_row.rearrange("p (t b) -> p t b", b=BATCH).unsqueeze(3).to_broadcast([P, Q, BATCH, Q]),
                                       spread(T.mask4[:], [[0, Q], [0, BATCH], [1, Q]]), ALU.mult).then_inc(cb_made, 1)

                def two_quads(n):
                    for h in range(2):
                        expand_b(n * 2 + h + 2, h)
                        expand_c(n * 2 + h, h)

                add_bias(0)
                expand_b(0, 0)
                expand_b(1, 1)
                two_quads(0)
                with pool.Fori(1, 7) as n:
                    two_quads(n)
                add_bias(1)
                two_quads(7)
                with pool.Fori(1, NCH - 1) as k:
                    with pool.Fori(0, 7) as n:
                        two_quads(k * 8 + n)
                    add_bias(k + 1)
                    two_quads(k * 8 + 7)
                with pool.Fori((NCH - 1) * 8, NCH * 8 - 1) as n:
                    two_quads(n)
                for h in range(2):
                    expand_c(QUADS - 2 + h, h)

            @block.vector
            def _(dve):
                decay = spread(T.decay[:], [[0, Q], [1, ST]])
                by_b = lambda t: t.rearrange("p (b g) -> p b g", g=ST)

                def eight_steps(n):
                    for r in range(2 * Q):
                        t = n * 8 + r
                        start = isinstance(n, int) and t == 0
                        old, new = (r - 1) % (2 * Q), r
                        for half in range(GRP):
                            if start:
                                dve.wait_ge(zeroed, 1)
                            else:
                                dve.wait_ge(steps, t * 6 - 1 + half)
                            dve.tensor_tensor(by_b(scaled[:, half, :]), by_b(state[:, old, half, :]), decay,
                                              ALU.mult).then_inc(steps, 1)
                        if r % 2 == 0:
                            dve.wait_ge(u_made, n * 4 + r // 2 + 1)
                        for half in range(GRP):
                            dve.wait_ge(steps, t * 6 + 1 + half)
                            at = r % 2 * 256 + half * HALF
                            dve.tensor_tensor(summed[:, half, :], scaled[:, half, :], u_bank[r // 2][:, at:at + HALF],
                                              ALU.add).then_inc(steps, 1)
                        if r % Q == 0 and not isinstance(n, int):
                            dve.wait_ge(y_made, n * 2 + r // Q - 1)
                        for half in range(GRP):
                            dve.wait_ge(steps, t * 6 + 3 + half)
                            dve.tensor_scalar(state[:, new, half, :], summed[:, half, :], 10.0, -10.0, ALU.min, ALU.max).then_inc(steps, 1)

                eight_steps(0)
                with dve.Fori(1, NCH * 8) as n:
                    eight_steps(n)


def repeat_outer(ap, n):
    return ap.unsqueeze(1).to_broadcast([ap.shape[0], n, ap.shape[1]])


def project_out(nc, T):
    with ExitStack() as ctx:
        swapped, gated, made, taken, biased = (ctx.enter_context(nc.semaphore("po_" + name)) for name in ("swapped", "gated", "made", "taken", "biased"))
        HL = Q * L
        turned = T.share[:, 0:GRP * HL].rearrange("p (h n t q) -> p h q n t", h=GRP, t=2 * Q, q=Q)
        with nc.Block() as block:
            @block.vector
            def _(dve):
                for half in range(GRP):
                    dve.transpose(T.share[:, half * HL:(half + 1) * HL], T.xt[:, half * HL:(half + 1) * HL]).then_inc(swapped, 1)
                for half in range(GRP):
                    dve.wait_ge(swapped, half + 1)
                    z = T.zq[:, half, :, :].rearrange("p q (n t) -> p q n t", t=2 * Q)
                    for dq in range(Q):
                        dve.tensor_tensor(z[:, dq], turned[:, half, dq], z[:, dq], ALU.mult).then_inc(gated, 1)
                dve.wait_ge(biased, 1)
                for b in range(BATCH):
                    dve.wait_ge(made, b + 1)
                    part = T.xn[:, 4 * b:4 * b + 4, 0:D]
                    dve.tensor_tensor(part, T.bank[b % 4][:].rearrange("p (t d) -> p t d", d=D), part, ALU.add).then_inc(taken, 1)

            @block.gpsimd
            def _(pool):
                pool.tensor_tensor(T.xn[:, :, 0:D], T.xn[:, :, 0:D], spread(T.rows[:, 0, :], [[0, NT], [1, D]]), ALU.add).then_inc(biased, 1)

            @block.tensor
            def _(pe):
                for b in range(BATCH):
                    half, rows = b // Q, slice(ST * (b % Q), ST * (b % Q) + ST)
                    pe.wait_ge(gated, Q * (half + 1))
                    if b >= 4:
                        pe.wait_ge(taken, b - 3)
                    for tile in range(4):
                        for dq in range(Q):
                            last = pe.matmul(T.bank[b % 4][:, tile * D:(tile + 1) * D], T.zq[rows, half, dq, tile * P:(tile + 1) * P],
                                             T.o_q[rows, dq, :], start=(dq == 0), stop=(dq == Q - 1))
                    last.then_inc(made, 1)


def add_normalized(nc, T):
    PARTS = 4
    with ExitStack() as ctx:
        scaled, moved, added = (ctx.enter_context(nc.semaphore("an_" + name)) for name in ("scaled", "moved", "added"))
        with nc.Block() as block:
            @block.vector
            def _(dve):
                row = lambda k: spread(T.rows[:, k, :], [[0, NT // PARTS], [1, D]])
                parts = [slice(n * NT // PARTS, (n + 1) * NT // PARTS) for n in range(PARTS)]
                for part in parts:
                    dve.tensor_tensor(T.xn[:, part, 0:D], T.xn[:, part, 0:D], row(1), ALU.mult).then_inc(scaled, 1)
                for n, part in enumerate(parts):
                    dve.wait_ge(scaled, n + 1)
                    dve.tensor_tensor(T.x[:, part, :], T.x[:, part, :], row(2), ALU.add).then_inc(moved, 1)
                for n, part in enumerate(parts):
                    dve.wait_ge(moved, n + 1)
                    dve.tensor_tensor(T.x[:, part, :], T.x[:, part, :], T.xn[:, part, 0:D], ALU.add).then_inc(added, 1)


_INS = ["L0_attn_x", "L0_attn_in_w", "L0_attn_in_b", "L0_attn_conv_w", "L0_attn_conv_b", "L0_attn_A_log", "L0_attn_B_w",
        "L0_attn_B_b", "L0_attn_C_w", "L0_attn_C_b", "L0_attn_out_w", "L0_attn_out_b", "L0_attn_ln_w", "L0_attn_ln_b",
        "L0_ffn_Wr", "L0_ffn_W1", "L0_ffn_b1", "L0_ffn_W2", "L0_ffn_b2"]


def kernel(**inputs):
    import numpy as np
    import concourse.bacc as bacc
    from concourse.bass_utils import run_bass_kernel_spmd

    nc = bacc.Bacc("TRN2", target_bir_lowering=False, num_devices=1)
    arrays, args = {}, {}
    for name in _INS:
        array = np.ascontiguousarray(inputs[name])
        arrays[name] = array
        args[name] = nc.dram_tensor(name, array.shape, mybir.dt.from_np(array.dtype), kind="ExternalInput").ap()
    out = nc.dram_tensor("out", (BATCH, L, D), F32, kind="ExternalOutput").ap()
    build(nc, args, out)
    results = run_bass_kernel_spmd(nc, [arrays], core_ids=[0])
    return results.results[0]["out"]
```

```python
from contextlib import ExitStack

import concourse.bass as bass
from concourse import mybir

F32 = mybir.dt.float32
BF16 = mybir.dt.bfloat16
I32 = mybir.dt.int32
U32 = mybir.dt.uint32
ALU = mybir.AluOpType
ACT = mybir.ActivationFunctionType
AX = mybir.AxisListType

P = 128
BATCH, L, D = 8, 512, 128
TOK = BATCH * L
NT = TOK // P
E, F = 8, 512
FC = F // P
ST = 32
USED = TOK // P + E - 1
TILES = 40
SLOTS = TILES * P
EPS = 1e-5
WROW = FC * P + FC * P + FC + D
W2_AT, B1_AT, B2_AT = F, 2 * F, 2 * F + FC
Q = 4
CH = 64
NCH = L // CH
GRP = 2
HALF = BATCH // GRP * ST
QUADS = L // Q
RING = 10
GROUPS, GT = 4, NT // 4
ROW_GROUPS = [slice(g * GT, (g + 1) * GT) for g in range(GROUPS)]
TIME_GROUPS = [slice(g, NT, L // P) for g in range(GROUPS)]
LOGITS = 6


def spread(ap, dims):
    return bass.AP(tensor=ap.tensor, offset=ap.offset, ap=[list(ap.ap[0])] + [list(d) for d in dims])


class Tensors:
    pass


def build(nc, a, out):
    with ExitStack() as ctx:
        def sb(name, shape, dt=F32):
            return ctx.enter_context(nc.sbuf_tensor(name, shape, dt))

        def dram(name, shape):
            return nc.dram_tensor(name, shape, F32, kind="Internal").ap()

        T = Tensors()
        T.x = sb("x", [P, NT, D])
        T.xn = sb("xn", [P, NT, D])
        T.xt = sb("xt", [P, NT, P])
        T.tables = sb("tables", [P, E, WROW])
        T.ident = sb("ident", [P, P])
        T.since = sb("since", [P, P], BF16)
        T.all_ones = sb("all_ones", [P, P], BF16)
        T.ones = sb("ones", [P, P])
        T.wr = sb("wr", [P, E])
        T.tile_expert = sb("tile_expert", [P, TILES], I32)
        T.take_from = sb("take_from", [P, TILES], U32)
        T.give_to = sb("give_to", [P, TILES], U32)
        T.gate = sb("gate", [P, NT])
        T.share = sb("share", [P, 2 * CH // Q * BATCH * ST])
        T.in_t = sb("in_t", [P, 2 * D])
        T.b_t = sb("b_t", [P, ST])
        T.c_rep = sb("c_rep", [P, Q, ST])
        T.o_t = sb("o_t", [P, D])
        T.conv_diag = sb("conv_diag", [P, Q, P])
        T.cols = sb("cols", [P, 4])
        T.rows = sb("rows", [P, 3, D])
        T.bb_row = sb("bb_row", [P, ST])
        T.decay = sb("decay", [P, ST])
        T.mask4 = sb("mask4", [P, Q])
        T.mask8 = sb("mask8", [P, BATCH])
        T.mask16 = sb("mask16", [P, Q * Q])
        T.stack = sb("stack", [P, ST])
        T.z = sb("z", [P, 2, BATCH * CH])
        T.yt = sb("yt", [P, GRP, CH * Q])
        T.xa = sb("xa", [P, BATCH, L + 4])
        T.tokens = [dram(f"tokens{n}", [TOK, D]) for n in range(2)]
        T.ffn_out = [dram(f"ffn_out{n}", [TOK + SLOTS, D]) for n in range(2)]
        T.bank = [ctx.enter_context(nc.psum_tensor(f"bank{n}", [P, 512], F32)) for n in range(8)]

        T.x_in = [ctx.enter_context(nc.semaphore(f"x_in{n}")) for n in range(4)]
        T.tables_in, T.small_in = (ctx.enter_context(nc.semaphore(name)) for name in ("tables_in", "small_in"))
        T.rows_loaded = [ctx.enter_context(nc.semaphore(f"rows_loaded{r}")) for r in range(RING)]
        T.outs_stored = [ctx.enter_context(nc.semaphore(f"outs_stored{r}")) for r in range(RING)]
        T.y_moved = ctx.enter_context(nc.semaphore("y_moved"))
        T.tokens_out = [ctx.enter_context(nc.semaphore(f"tokens_out{n}")) for n in range(2)]

        first_normalization(nc, T, a)
        route(nc, T, "r0_")
        experts(nc, T, "e0_", 0)
        enter_attention(nc, T)
        scan(nc, T)
        finish_attention(nc, T)
        route(nc, T, "r1_")
        experts(nc, T, "e1_", 1)
        last_sum(nc, T, out)
    return nc


class Normalization:

    def __init__(self, ctx, nc, T, tag, v, groups):
        sem = lambda name: ctx.enter_context(nc.semaphore(tag + name))
        self.nc, self.T, self.v, self.groups = nc, T, v, groups
        self.tiles = [list(range(*group.indices(NT))) for group in groups]
        self.stats_made, self.aggregated, self.roots_made, self.inverses, self.shifts = map(
            sem, ("stats_made", "aggregated", "roots_made", "inverses", "shifts"))
        self.raw, self.stat, self.var, self.root, self.rstd, self.shift = (
            ctx.enter_context(nc.sbuf_tensor(tag + name, shape, F32)) for name, shape in (
                ("raw", [P, NT, 6]), ("stat", [P, NT, 2]), ("var", [P, NT]), ("root", [P, NT]), ("rstd", [P, NT]), ("shift", [P, NT])))
        self.normed, self.act_normed, self.transposed, self.xt_made = map(
            sem, ("normed", "act_normed", "transposed", "xt_made"))

    def take_stats(self, dve, g):
        for j in self.tiles[g]:
            dve.bn_stats(self.raw[:, j, :], self.v[:, j, :]).then_inc(self.stats_made, 1)

    def aggregate(self, dve, g):
        T, group = self.T, self.groups[g]
        for n, j in enumerate(self.tiles[g]):
            dve.wait_ge(self.stats_made, g * GT + n + 1)
            dve.bn_aggr(self.stat[:, j, :], self.raw[:, j, :]).then_inc(self.aggregated, 1)
        dve.wait_ge(self.aggregated, g * (GT + 1) + GT)
        dve.tensor_scalar(self.var[:, group], self.stat[:, group, 1], EPS, None, ALU.add).then_inc(self.aggregated, 1)

    def take_root(self, act, g):
        act.wait_ge(self.aggregated, (g + 1) * (GT + 1))
        act.activation(self.root[:, self.groups[g]], self.var[:, self.groups[g]], ACT.Sqrt).then_inc(self.roots_made, 1)

    def invert(self, dve, g):
        T, group = self.T, self.groups[g]
        dve.wait_ge(self.roots_made, g + 1)
        rstd, tmp, var = self.rstd[:, group], self.root[:, group], self.var[:, group]
        dve.reciprocal(rstd, tmp).then_inc(self.inverses, 1)
        dve.wait_ge(self.inverses, 4 * g + 1)
        dve.tensor_tensor(tmp, var, rstd, ALU.mult).then_inc(self.inverses, 1)
        dve.wait_ge(self.inverses, 4 * g + 2)
        dve.scalar_tensor_tensor(tmp, tmp, -0.5, rstd, ALU.mult, ALU.mult).then_inc(self.inverses, 1)
        dve.wait_ge(self.inverses, 4 * g + 3)
        dve.scalar_tensor_tensor(rstd, tmp, 1.5, rstd, ALU.add, ALU.mult).then_inc(self.inverses, 1)
        dve.wait_ge(self.inverses, 4 * g + 4)
        dve.scalar_tensor_tensor(self.shift[:, group], self.stat[:, group, 0], -1.0, self.rstd[:, group],
                                 ALU.mult, ALU.mult).then_inc(self.shifts, 1)

    DVE_SHARE, ACT_SHARE = (0, 1, 3, 4, 6), (2, 5, 7)

    def normalize_dve(self, dve, g):
        T = self.T
        for n in self.DVE_SHARE:
            j = self.tiles[g][n]
            dve.tensor_scalar(T.xn[:, j, :], self.v[:, j, :], self.stat[:, j, 0:1], self.rstd[:, j:j + 1],
                              ALU.subtract, ALU.mult).then_inc(self.normed, 1)

    def normalize_act(self, act, g, share=ACT_SHARE):
        T = self.T
        act.wait_ge(self.shifts, g + 1)
        for n in share:
            j = self.tiles[g][n]
            act.activation(T.xn[:, j, :], self.v[:, j, :], ACT.Identity, scale=self.rstd[:, j:j + 1],
                           bias=self.shift[:, j:j + 1]).then_inc(self.act_normed, 1)

    def transpose(self, pe, g, banks):
        T = self.T
        for half in range(2):
            for n in range(4 * half, 4 * half + 4):
                if n in self.DVE_SHARE:
                    pe.wait_ge(self.normed, g * len(self.DVE_SHARE) + self.DVE_SHARE.index(n) + 1)
                else:
                    pe.wait_ge(self.act_normed, g * len(self.ACT_SHARE) + self.ACT_SHARE.index(n) + 1)
                if g >= len(banks) // 2 and n == 4 * half:
                    pe.wait_ge(self.xt_made, g * 2 + half + 1 - len(banks))
                last = pe.transpose(banks[(2 * g + half) % len(banks)][:, n % 4 * P:(n % 4 + 1) * P], T.xn[:, self.tiles[g][n], :], T.ident[:])
            last.then_inc(self.transposed, 1)

    def take_transposed(self, act, g, banks):
        for half in range(2):
            act.wait_ge(self.transposed, g * 2 + half + 1)
            tiles = self.tiles[g][4 * half:4 * half + 4]
            act.activation(self.T.xt[:, tiles[0]:tiles[3] + 1:tiles[1] - tiles[0], :],
                           banks[(2 * g + half) % len(banks)][:].rearrange("p (j t) -> p j t", t=P), ACT.Copy).then_inc(self.xt_made, 1)

    def logits(self, pe, g):
        T = self.T
        pe.wait_ge(self.xt_made, g * 2 + 2)
        for j in self.tiles[g]:
            pe.matmul(T.bank[LOGITS][:, j * E:(j + 1) * E], T.xt[:, j, :], T.wr[:], start=True, stop=True)

    def store_tokens(self, sp, ffn):
        T = self.T
        rows = T.tokens[ffn].rearrange("(j p) d -> p j d", p=P)
        for g, group in enumerate(self.groups):
            sp.wait_ge(self.normed, (g + 1) * len(self.DVE_SHARE))
            sp.wait_ge(self.act_normed, (g + 1) * len(self.ACT_SHARE))
            sp.dma_start(rows[:, group, :], T.xn[:, group, :]).then_inc(T.tokens_out[ffn], 16)


def first_normalization(nc, T, a):
    with ExitStack() as ctx:
        def sem(name):
            return ctx.enter_context(nc.semaphore("s_" + name))

        def sb(name, shape, dt=F32):
            return ctx.enter_context(nc.sbuf_tensor("s_" + name, shape, dt))

        w_in, pool_made, dve_made, pe_made, act_made = map(sem, ("w_in", "pool_made", "dve_made", "pe_made", "act_made"))
        in_w = sb("in_w", [P, 2, D])
        bc_w = sb("bc_w", [2 * ST, D])
        out_w = sb("out_w", [P, D])
        b1 = sb("b1", [E * FC, P])
        taps = sb("taps", [P, Q])
        a_log = sb("a_log", [P, ST])
        a_t = sb("a_t", [P, ST])
        N = Normalization(ctx, nc, T, "n0_", T.x, ROW_GROUPS)
        banks = [T.bank[n] for n in (3, 4, 5, 7)]

        with nc.Block() as block:
            @block.sync
            def _(sp):
                x = a["L0_attn_x"].rearrange("b (q p) d -> p (b q) d", p=P)
                for g, group in enumerate(ROW_GROUPS):
                    sp.dma_start(T.x[:, group, :], x[:, group, :]).then_inc(T.x_in[g], 16)
                sp.dma_start(in_w[:], a["L0_attn_in_w"].rearrange("(h p) c -> p h c", p=P)).then_inc(w_in, 16)
                sp.dma_start(bc_w[0:ST, :], a["L0_attn_B_w"]).then_inc(w_in, 16)
                sp.dma_start(bc_w[ST:2 * ST, :], a["L0_attn_C_w"]).then_inc(w_in, 16)
                sp.dma_start(out_w[:], a["L0_attn_out_w"]).then_inc(w_in, 16)
                sp.dma_start(T.tables[:, :, 0:F], a["L0_ffn_W1"].rearrange("e d f -> d e f")).then_inc(T.tables_in, 16)
                for e in range(E):
                    sp.dma_start(T.tables[:, e, W2_AT:W2_AT + F].rearrange("p (c d) -> p c d", d=D),
                                 a["L0_ffn_W2"][e].rearrange("(c p) d -> p c d", p=P)).then_inc(T.tables_in, 16)
                sp.dma_start(T.tables[:, :, B2_AT:B2_AT + D],
                             bass.AP(tensor=a["L0_ffn_b2"].tensor, offset=0, ap=[[0, P], [D, E], [1, D]])).then_inc(T.tables_in, 16)
                for k, name in enumerate(("L0_attn_out_b", "L0_attn_ln_w", "L0_attn_ln_b")):
                    sp.dma_start(T.rows[:, k, :], bass.AP(tensor=a[name].tensor, offset=0, ap=[[0, P], [1, D]])).then_inc(T.small_in, 16)
                sp.dma_start(T.bb_row[:], bass.AP(tensor=a["L0_attn_B_b"].tensor, offset=0, ap=[[0, P], [1, ST]])).then_inc(T.small_in, 16)
                column = lambda name, at, n=P: bass.AP(tensor=a[name].tensor, offset=at, ap=[[1, n], [1, 1]])
                sp.dma_start(T.cols[:, 0:1], column("L0_attn_in_b", 0)).then_inc(T.small_in, 16)
                sp.dma_start(T.cols[:, 1:2], column("L0_attn_in_b", D)).then_inc(T.small_in, 16)
                sp.dma_start(T.cols[:, 2:3], column("L0_attn_conv_b", 0)).then_inc(T.small_in, 16)
                for b in range(Q):
                    sp.dma_start(T.cols[ST * b:ST * b + ST, 3:4], column("L0_attn_C_b", 0, n=ST)).then_inc(T.small_in, 16)
                N.store_tokens(sp, 0)

            @block.scalar
            def _(act):
                act.dma_start(b1[:], a["L0_ffn_b1"].rearrange("e (c p) -> (e c) p", p=P)).then_inc(w_in, 16)
                act.dma_start(taps[:], a["L0_attn_conv_w"].rearrange("c o k -> c (o k)")).then_inc(w_in, 16)
                act.dma_start(a_log[:], a["L0_attn_A_log"]).then_inc(w_in, 16)
                act.dma_start(T.wr[:], a["L0_ffn_Wr"]).then_inc(w_in, 16)
                for g in range(GROUPS):
                    N.take_root(act, g)
                    N.normalize_act(act, g)
                    if g >= 1:
                        N.take_transposed(act, g - 1, banks)
                N.take_transposed(act, GROUPS - 1, banks)
                act.wait_ge(dve_made, 2)
                act.activation(T.decay[:], a_t[:], ACT.Exp).then_inc(act_made, 1)

            @block.gpsimd
            def _(pool):
                pool.memset(T.ones[:], 1.0).then_inc(pool_made, 1)
                pool.wait_ge(pool_made, 1)
                pool.affine_select(out=T.ident[:], in_=T.ones[:], compare_op=ALU.is_equal, fill=0.0,
                                   base=0, pattern=[[-1, P]], channel_multiplier=1).then_inc(pool_made, 1)
                pool.memset(T.all_ones[:], 1.0).then_inc(pool_made, 1)
                pool.memset(T.since[:], -1.0).then_inc(pool_made, 1)
                pool.wait_ge(pool_made, 4)
                pool.affine_select(out=T.since[:], in_=T.since[:], compare_op=ALU.is_ge, fill=0.0,
                                   base=0, pattern=[[-1, P]], channel_multiplier=1).then_inc(pool_made, 1)
                pool.memset(T.xa[:, :, 0:2], 0.0).then_inc(pool_made, 1)
                pool.memset(T.xa[:, :, L + 2:L + 4], 0.0).then_inc(pool_made, 1)

            @block.vector
            def _(dve):
                def operands():
                    dve.wait_ge(pool_made, 2)
                    dve.wait_ge(w_in, 16 * 8)
                    dve.tensor_scalar(a_log[:], a_log[:], -5.0, 2.0, ALU.max, ALU.min).then_inc(dve_made, 1)
                    dve.wait_ge(dve_made, 1)
                    dve.transpose(a_t[:], a_log[:]).then_inc(dve_made, 1)
                    ident = T.ident[:]
                    dve.tensor_reduce(T.mask4[:], ident.rearrange("p (i k) -> p i k", i=Q), AX.X, ALU.add).then_inc(dve_made, 1)
                    dve.tensor_reduce(T.mask16[:], ident.rearrange("p (i k) -> p i k", i=Q * Q), AX.X, ALU.add).then_inc(dve_made, 1)
                    dve.tensor_reduce(T.mask8[:], ident.rearrange("p (k i) -> p i k", i=BATCH), AX.X, ALU.add).then_inc(dve_made, 1)
                    dve.tensor_reduce(T.stack[:], ident.rearrange("p (k i) -> p i k", i=ST), AX.X, ALU.add).then_inc(dve_made, 1)
                    for k in range(Q):
                        dve.tensor_scalar(T.conv_diag[:, k, :], ident, taps[:, k:k + 1], None, ALU.mult).then_inc(dve_made, 1)
                    dve.wait_ge(pe_made, 1)
                    dve.tensor_copy(T.in_t[:], T.bank[0][:, 0:2 * D]).then_inc(dve_made, 1)
                    dve.tensor_copy(T.b_t[:], T.bank[1][:, 0:ST]).then_inc(dve_made, 1)
                    dve.tensor_copy(T.c_rep[:], spread(T.bank[1][:, ST:2 * ST], [[0, Q], [1, ST]])).then_inc(dve_made, 1)
                    dve.tensor_copy(T.tables[:, :, B1_AT:B1_AT + FC],
                                    T.bank[2][:, 0:E * FC].rearrange("p (e c) -> p e c", c=FC)).then_inc(dve_made, 1)
                    dve.tensor_copy(T.o_t[:], T.bank[2][:, D:2 * D]).then_inc(dve_made, 1)

                for g in range(GROUPS):
                    dve.wait_ge(T.x_in[g], 16)
                    N.take_stats(dve, g)
                    N.aggregate(dve, g)
                    N.invert(dve, g)
                    N.normalize_dve(dve, g)
                operands()
                dve.wait_ge(act_made, 1)
                dve.tensor_scalar(T.decay[:], T.decay[:], -1.0, None, ALU.mult).then_inc(dve_made, 1)

            @block.tensor
            def _(pe):
                pe.wait_ge(pool_made, 2)
                N.transpose(pe, 0, banks)
                pe.wait_ge(w_in, 16 * 8)
                for h in range(2):
                    pe.transpose(T.bank[0][:, h * D:(h + 1) * D], in_w[:, h, :], T.ident[:])
                pe.transpose(T.bank[1][:, 0:2 * ST], bc_w[:], T.ident[0:2 * ST, 0:2 * ST])
                pe.transpose(T.bank[2][:, 0:E * FC], b1[:], T.ident[0:E * FC, 0:E * FC])
                pe.transpose(T.bank[2][:, D:2 * D], out_w[:], T.ident[:]).then_inc(pe_made, 1)
                for g in range(GROUPS):
                    if g + 1 < GROUPS:
                        N.transpose(pe, g + 1, banks)
                    N.logits(pe, g)


def enter_attention(nc, T):
    with ExitStack() as ctx:
        N = Normalization(ctx, nc, T, "nb_", T.x, ROW_GROUPS)
        R = Residual(ctx, nc, T, "rb_", T.ffn_out[0])
        banks = T.bank[4:6]
        in_made, in_taken = (ctx.enter_context(nc.semaphore("in_" + name)) for name in ("made", "taken"))
        with nc.Block() as block:
            @block.sync
            def _(sp):
                R.load(sp)

            @block.vector
            def _(dve):
                for g in range(GROUPS + 1):
                    if g < GROUPS:
                        R.add_dve(dve, g)
                        dve.wait_ge(R.added, (g + 1) * len(R.DVE_SHARE))
                        dve.wait_ge(R.pool_added, g + 1)
                        N.take_stats(dve, g)
                        N.aggregate(dve, g)
                    if g >= 1:
                        N.invert(dve, g - 1)
                        N.normalize_dve(dve, g - 1)

            @block.gpsimd
            def _(pool):
                for g in range(GROUPS):
                    R.add_pool(pool, g)

            @block.scalar
            def _(act):
                N.take_root(act, 0)
                for g in range(GROUPS):
                    if g + 1 < GROUPS:
                        N.take_root(act, g + 1)
                    N.normalize_act(act, g)
                    N.take_transposed(act, g, banks)
                    if g == 0:
                        act.wait_ge(T.small_in, 16 * (7 + Q))
                    for b in range(2 * g, 2 * g + 2):
                        act.wait_ge(in_made, b + 1)
                        act.activation(T.xa[:, b, 2:2 + L], T.bank[b % 4][:], ACT.Identity, bias=T.cols[:, 0:1]).then_inc(in_taken, 1)

            @block.tensor
            def _(pe):
                for g in range(GROUPS):
                    N.transpose(pe, g, banks)
                    pe.wait_ge(N.xt_made, 2 * g + 2)
                    for b in range(2 * g, 2 * g + 2):
                        if b >= 4:
                            pe.wait_ge(in_taken, b - 3)
                        pe.matmul(T.bank[b % 4][:], T.in_t[:, 0:D], by_channel(T)[:, b, :], start=True, stop=True).then_inc(in_made, 1)


def route(nc, T, tag):
    with ExitStack() as ctx:
        def sem(name):
            return ctx.enter_context(nc.semaphore(tag + name))

        def sb(name, shape, dt=F32):
            return ctx.enter_context(nc.sbuf_tensor(tag + name, shape, dt))

        chain, exps_made, counted, const_made, where_made, tile_made, low_made, pool_low_made, low_used = map(
            sem, ("chain", "exps_made", "counted", "const_made", "where_made", "tile_made", "low_made", "pool_low_made", "low_used"))
        by_pool = [j % 5 == 4 for j in range(NT)]
        logits = sb("logits", [P, E, NT])
        exps = sb("exps", [P, E, NT])
        pick = sb("pick", [P, E, NT], BF16)
        place = sb("place", [P, E, NT])
        upto = sb("upto", [P, E, NT])
        carry = sb("carry", [P, E, NT])
        best = sb("best", [P, NT])
        total = sb("total", [P, NT])
        rank_e = sb("rank_e", [P, E])
        count = sb("count", [P, E], I32)
        tiles = sb("tiles", [P, E])
        ends = sb("ends", [P, E])
        base = sb("base", [P, E])
        tile_no = sb("tile_no", [P, TILES])
        past = sb("past", [P, TILES, E])
        tile_e = sb("tile_e", [P, TILES])
        slot = sb("slot", [P, NT], I32)
        high = sb("high", [P, NT], I32)
        high_f = sb("high_f", [P, NT])
        low_f = sb("low_f", [P, NT])
        token = sb("token", [P, 1])
        tile = sb("tile", [P, NT])
        lane = sb("lane", [P, P])
        spare = sb("spare", [P, TILES])
        LOWS = 16
        low = [sb(f"low{r}", [P, P], BF16) for r in range(LOWS)]
        where = sb("where", [P, NT, 3, TILES], BF16)
        took = sb("took", [P, TILES])
        empty = sb("empty", [P, TILES])

        by_tile = lambda t: t[:].rearrange("p e j -> p j e")
        over_e = lambda t: spread(t[:], [[0, E], [1, NT]])
        over_j = lambda t: spread(t[:], [[1, E], [0, NT]])

        with nc.Block() as block:
            @block.gpsimd
            def _(pool):
                exact = dict(allow_small_or_imprecise_dtypes=True)
                pool.memset(carry[:], 1.0).then_inc(const_made, 1)
                pool.iota(rank_e[:], pattern=[[-1, E]], base=E, channel_multiplier=0, **exact).then_inc(const_made, 1)
                pool.iota(tile_no[:], pattern=[[1, TILES]], base=0, channel_multiplier=0, **exact).then_inc(const_made, 1)
                pool.iota(token[:], pattern=[[0, 1]], base=0, channel_multiplier=1, **exact).then_inc(const_made, 1)
                pool.iota(tile[:], pattern=[[1, NT]], base=0, channel_multiplier=0, **exact).then_inc(const_made, 1)
                pool.iota(lane[:], pattern=[[1, P]], base=0, channel_multiplier=0, **exact).then_inc(const_made, 1)
                pool.iota(spare[:], pattern=[[P, TILES]], base=TOK, channel_multiplier=1, **exact).then_inc(const_made, 1)
                pool.wait_ge(const_made, 7)
                pool.memset(carry[:, :, 0:1], 0.0).then_inc(const_made, 1)
                pool.wait_ge(where_made, 1)
                pool.tensor_tensor(where[:, :, 2, :], where[:, :, 1, :], spread(tile[:], [[1, NT], [0, TILES]]),
                                   ALU.mult).then_inc(tile_made, 1)
                for j in range(NT):
                    if by_pool[j]:
                        if j >= LOWS:
                            pool.wait_ge(low_used, j - LOWS + 1)
                        pool.tensor_scalar(low[j % LOWS][:], lane[:], low_f[:, j:j + 1], None, ALU.is_equal).then_inc(pool_low_made, 1)

            @block.scalar
            def _(act):
                act.wait_ge(chain, 3)
                act.activation(exps[:], logits[:], ACT.Exp).then_inc(exps_made, 1)

            @block.tensor
            def _(pe):
                pe.wait_ge(chain, 6)
                pe.matmul(T.bank[0][:, 0:E * NT], T.since[:], pick[:].rearrange("p e j -> p (e j)"), start=True, stop=True)
                pe.matmul(T.bank[1][:, 0:E * NT], T.all_ones[:], pick[:].rearrange("p e j -> p (e j)"),
                          start=True, stop=True).then_inc(counted, 1)
                pe.wait_ge(where_made, 2)
                pe.wait_ge(tile_made, 1)
                for j in range(NT):
                    if by_pool[j]:
                        pe.wait_ge(pool_low_made, sum(by_pool[:j + 1]))
                    else:
                        pe.wait_ge(low_made, j + 1 - sum(by_pool[:j + 1]))
                    pe.matmul(T.bank[2][:, 0:3 * TILES], low[j % LOWS][:], where[:, j, :, :].rearrange("p k i -> p (k i)"),
                              start=(j == 0), stop=(j == NT - 1)).then_inc(low_used, 1)

            @block.vector
            def _(dve):
                done = [0]

                def then(instruction):
                    done[0] += 1
                    instruction.then_inc(chain, 1)
                    dve.wait_ge(chain, done[0])

                then(dve.tensor_copy(logits[:], T.bank[LOGITS][:, 0:E * NT].rearrange("p (j e) -> p e j", e=E)))
                then(dve.tensor_reduce(best[:], by_tile(logits), AX.X, ALU.max))
                then(dve.tensor_tensor(logits[:], logits[:], over_e(best), ALU.subtract))
                dve.wait_ge(const_made, 8)
                then(dve.scalar_tensor_tensor(pick[:], logits[:], 0.0, over_j(rank_e), ALU.is_equal, ALU.mult))
                then(dve.tensor_reduce(best[:], by_tile(pick), AX.X, ALU.max))
                then(dve.tensor_tensor(pick[:], pick[:], over_e(best), ALU.is_equal))
                dve.wait_ge(exps_made, 1)
                then(dve.tensor_reduce(total[:], by_tile(exps), AX.X, ALU.add))
                then(dve.reciprocal(T.gate[:], total[:]))
                then(dve.tensor_scalar(T.gate[:], T.gate[:], 0.5, None, ALU.mult))
                dve.wait_ge(counted, 1)
                flat = lambda t: t[:].rearrange("p e j -> p (e j)")
                then(dve.tensor_tensor_scan(flat(upto), flat(carry), T.bank[1][:, 0:E * NT], 0.0, ALU.mult, ALU.add))
                then(dve.tensor_tensor(flat(place), flat(upto), T.bank[0][:, 0:E * NT], ALU.add))
                then(dve.tensor_scalar(count[:], upto[:, :, NT - 1], float(P - 1), None, ALU.add))
                then(dve.tensor_scalar(count[:], count[:], P.bit_length() - 1, None, ALU.arith_shift_right))
                then(dve.tensor_copy(tiles[:], count[:]))
                then(dve.tensor_tensor_scan(ends[:], T.ones[:, 0:E], tiles[:], 0.0, ALU.mult, ALU.add))
                then(dve.tensor_tensor(base[:], ends[:], tiles[:], ALU.subtract))
                then(dve.tensor_scalar(base[:], base[:], float(P), None, ALU.mult))
                then(dve.tensor_tensor(place[:], place[:], over_j(base), ALU.add))
                then(dve.tensor_tensor(place[:], place[:], pick[:], ALU.mult))
                then(dve.tensor_reduce(best[:], by_tile(place), AX.X, ALU.add))
                then(dve.tensor_copy(slot[:], best[:]))
                then(dve.tensor_scalar(high[:], slot[:], P.bit_length() - 1, None, ALU.arith_shift_right))
                then(dve.tensor_copy(high_f[:], high[:]))
                then(dve.scalar_tensor_tensor(low_f[:], high_f[:], float(-P), best[:], ALU.mult, ALU.add))
                dve.tensor_tensor(where[:, :, 1, :], spread(tile_no[:], [[0, NT], [1, TILES]]),
                                  spread(high_f[:], [[1, NT], [0, TILES]]), ALU.is_equal).then_inc(where_made, 1)
                dve.wait_ge(where_made, 1)
                dve.tensor_scalar(where[:, :, 0, :], where[:, :, 1, :], token[:], None, ALU.mult).then_inc(where_made, 1)
                then(dve.tensor_tensor(past[:], spread(tile_no[:], [[1, TILES], [0, E]]),
                                       spread(ends[:], [[0, TILES], [1, E]]), ALU.is_ge))
                then(dve.tensor_reduce(tile_e[:], past[:], AX.X, ALU.add))
                then(dve.tensor_scalar(T.tile_expert[:], tile_e[:], float(E - 1), None, ALU.min))
                for j in range(NT):
                    if not by_pool[j]:
                        if j >= LOWS:
                            dve.wait_ge(low_used, j - LOWS + 1)
                        dve.tensor_scalar(low[j % LOWS][:], lane[:], low_f[:, j:j + 1], None, ALU.is_equal).then_inc(low_made, 1)
                dve.wait_ge(low_used, NT)
                then(dve.tensor_copy(took[:], T.bank[2][:, 0:TILES]))
                then(dve.scalar_tensor_tensor(took[:], T.bank[2][:, 2 * TILES:3 * TILES], float(P), took[:], ALU.mult, ALU.add))
                then(dve.tensor_copy(T.take_from[:], took[:]))
                then(dve.tensor_tensor(empty[:], spare[:], T.bank[2][:, TILES:2 * TILES], ALU.mult))
                then(dve.tensor_tensor(empty[:], spare[:], empty[:], ALU.subtract))
                then(dve.tensor_tensor(T.give_to[:], empty[:], took[:], ALU.add))


def experts(nc, T, tag, ffn):
    tokens, tokens_out, ffn_out = T.tokens[ffn], T.tokens_out[ffn], T.ffn_out[ffn]
    STAGES = TILES // RING
    AHEAD = 5
    with ExitStack() as ctx:
        def sem(name):
            return ctx.enter_context(nc.semaphore(tag + name))

        def sb(name, shape, dt=F32):
            return ctx.enter_context(nc.sbuf_tensor(tag + name, shape, dt))

        loaded, stored = T.rows_loaded, T.outs_stored
        in_place = lambda r: 16 * len(range(r, USED, RING))
        before = lambda r: ffn * in_place(r)
        turned, x_made, w_made, up_made, h_made, down_made, out_made = map(
            sem, ("turned", "x_made", "w_made", "up_made", "h_made", "down_made", "out_made"))
        rows = [sb(f"rows{r}", [P, D]) for r in range(RING)]
        outs = [sb(f"outs{r}", [P, D]) for r in range(RING)]
        xt = [sb(f"xt{r}", [P, P]) for r in range(AHEAD)]
        weights = [sb(f"weights{r}", [P, WROW]) for r in range(AHEAD)]
        hidden = [sb(f"hidden{r}", [P, FC, P]) for r in range(2)]
        turn, up, down = T.bank[0:2], T.bank[2:4], T.bank[4:6]

        def stages(eng, stage):
            stage(0, True, False, False)
            stage(1, False, True, False)
            with eng.Fori(2, STAGES - 1) as s:
                stage(s, False, False, False)
            stage(STAGES - 1, False, False, True)

        with nc.Block() as block:
            @block.tensor
            def _(pe):
                def turn_in(s, r, i, early):
                    pe.wait_ge(loaded[r], (s + 1) * 16 + before(r))
                    if not early:
                        pe.wait_ge(x_made, i - 1)
                    pe.transpose(turn[r % 2][:, 0:P], rows[r][:], T.ident[:]).then_inc(turned, 1)

                def go_up(i, r, early):
                    pe.wait_ge(x_made, i + 1)
                    pe.wait_ge(w_made, i + 1)
                    if not early:
                        pe.wait_ge(h_made, i - 1)
                    for c in range(FC):
                        last = pe.matmul(up[r % 2][:, c * P:(c + 1) * P], weights[r % AHEAD][:, c * P:(c + 1) * P],
                                         xt[r % AHEAD][:], start=True, stop=True)
                    last.then_inc(up_made, 1)

                def go_down(i, r, early):
                    pe.wait_ge(h_made, i + 1)
                    if not early:
                        pe.wait_ge(out_made, i - 1)
                    for c in range(FC):
                        last = pe.matmul(down[r % 2][:, 0:D], hidden[r % 2][:, c, :],
                                         weights[r % AHEAD][:, W2_AT + c * D:W2_AT + (c + 1) * D],
                                         start=(c == 0), stop=(c == FC - 1))
                    last.then_inc(down_made, 1)

                def stage(s, first, second, last):
                    for r in range(USED - s * RING if last else RING):
                        i = s * RING + r
                        if not (last and i + 2 >= USED):
                            turn_in(s + (r + 2) // RING, (r + 2) % RING, i + 2, False)
                        go_up(i, r, first and r < 2)
                        if not (first and r == 0):
                            go_down(i - 1, (r - 1) % RING, first and r < 3)

                turn_in(0, 0, 0, True)
                turn_in(0, 1, 1, True)
                stages(pe, stage)
                go_down(USED - 1, (USED - 1) % RING, False)

            @block.scalar
            def _(act):
                def stage(s, first, second, last):
                    for r in range(USED - s * RING if last else RING):
                        act.wait_ge(up_made, s * RING + r + 1)
                        for c in range(FC):
                            made = act.activation(hidden[r % 2][:, c, :], up[r % 2][:, c * P:(c + 1) * P], ACT.Gelu,
                                                  bias=weights[r % AHEAD][:, B1_AT + c:B1_AT + c + 1])
                        made.then_inc(h_made, 1)

                stages(act, stage)

            @block.vector
            def _(dve):
                def take_weights(i, r, early):
                    e = dve.value_load(T.tile_expert[0:1, bass.ds(i, 1)], min_val=0, max_val=E - 1)
                    if not early:
                        dve.wait_ge(down_made, i - AHEAD + 1)
                        dve.wait_ge(out_made, i - AHEAD + 1)
                    flat = T.tables[:].rearrange("p e w -> p (e w)")
                    dve.tensor_copy(weights[r % AHEAD][:], flat[:, bass.ds(e * WROW, WROW)]).then_inc(w_made, 1)

                def take_x(i, r):
                    dve.wait_ge(turned, i + 1)
                    dve.tensor_copy(xt[r % AHEAD][:], turn[r % 2][:, 0:P]).then_inc(x_made, 1)

                def give_out(s, i, r, early):
                    dve.wait_ge(down_made, i + 1)
                    if not early:
                        dve.wait_ge(stored[r], s * 16 + before(r))
                    dve.tensor_tensor(outs[r][:], down[r % 2][:, 0:D], weights[r % AHEAD][:, B2_AT:B2_AT + D],
                                      ALU.add).then_inc(out_made, 1)

                def stage(s, first, second, last):
                    for r in range(USED - s * RING if last else RING):
                        i = s * RING + r
                        if not (last and i + 2 >= USED):
                            take_x(i + 2, (r + 2) % RING)
                            take_weights(i + 2, (r + 2) % RING, first and r < 2)
                        if not (first and r == 0):
                            give_out(s - (r == 0), i - 1, (r - 1) % RING, first or (second and r == 0))

                dve.wait_ge(T.tables_in, 16 * (2 + E))
                for i in range(2):
                    take_x(i, i)
                    take_weights(i, i, True)
                stages(dve, stage)
                give_out(STAGES - 1, USED - 1, (USED - 1) % RING, False)

            @block.gpsimd
            def _(pool):
                LEAD = 9
                pool.wait_ge(tokens_out, 16 * 4)
                for i in range(USED + LEAD):
                    if i < USED:
                        if i >= RING:
                            pool.wait_ge(turned, i - RING + 1)
                        pool.indirect_dma_start(rows[i % RING][:], None, tokens,
                                                bass.IndirectOffsetOnAxis(ap=T.take_from[:, i:i + 1], axis=0)).then_inc(loaded[i % RING], 16)
                    if i >= LEAD:
                        n = i - LEAD
                        pool.wait_ge(out_made, n + 1)
                        pool.indirect_dma_start(ffn_out, bass.IndirectOffsetOnAxis(ap=T.give_to[:, n:n + 1], axis=0),
                                                outs[n % RING][:], None).then_inc(stored[n % RING], 16)
                for r in range(RING):
                    pool.wait_ge(stored[r], before(r) + in_place(r))


class Residual:
    DVE_SHARE, POOL_SHARE = (0, 1, 2, 3, 4, 5), (6, 7)

    def __init__(self, ctx, nc, T, tag, ffn_out):
        sem = lambda name: ctx.enter_context(nc.semaphore(tag + name))
        self.T, self.ffn_out = T, ffn_out
        self.loaded = [sem(f"loaded{g}") for g in range(GROUPS)]
        self.added, self.pool_scaled, self.pool_added = map(sem, ("added", "pool_scaled", "pool_added"))
        self.got = T.share[:, 0:NT * D].rearrange("p (j d) -> p j d", d=D)

    def load(self, sp):
        rows = self.ffn_out[0:TOK, :].rearrange("(j p) d -> p j d", p=P)
        for g, group in enumerate(ROW_GROUPS):
            sp.dma_start(self.got[:, group, :], rows[:, group, :]).then_inc(self.loaded[g], 16)

    def add_dve(self, dve, g):
        T = self.T
        dve.wait_ge(self.loaded[g], 16)
        for j in (g * GT + n for n in self.DVE_SHARE):
            dve.scalar_tensor_tensor(T.x[:, j, :], self.got[:, j, :], T.gate[:, j:j + 1], T.x[:, j, :],
                                     ALU.mult, ALU.add).then_inc(self.added, 1)

    def add_pool(self, pool, g):
        T = self.T
        pool.wait_ge(self.loaded[g], 16)
        part = slice(g * GT + self.POOL_SHARE[0], (g + 1) * GT)
        got, gates = self.got[:, part, :], spread(T.gate[:, part], [[1, len(self.POOL_SHARE)], [0, D]])
        pool.tensor_tensor(got, got, gates, ALU.mult).then_inc(self.pool_scaled, 1)
        pool.wait_ge(self.pool_scaled, g + 1)
        pool.tensor_tensor(T.x[:, part, :], T.x[:, part, :], got, ALU.add).then_inc(self.pool_added, 1)


def last_sum(nc, T, out):
    with ExitStack() as ctx:
        R = Residual(ctx, nc, T, "rl_", T.ffn_out[1])
        stored = ctx.enter_context(nc.semaphore("out_stored"))
        with nc.Block() as block:
            @block.sync
            def _(sp):
                R.load(sp)
                to = out.rearrange("b (q p) d -> p (b q) d", p=P)
                for g, group in enumerate(ROW_GROUPS):
                    sp.wait_ge(R.added, (g + 1) * len(R.DVE_SHARE))
                    sp.wait_ge(R.pool_added, g + 1)
                    sp.dma_start(to[:, group, :], T.x[:, group, :]).then_inc(stored, 16)
                sp.wait_ge(stored, 16 * GROUPS)

            @block.vector
            def _(dve):
                for g in range(GROUPS):
                    R.add_dve(dve, g)

            @block.gpsimd
            def _(pool):
                for g in range(GROUPS):
                    R.add_pool(pool, g)


def by_channel(T):
    return T.xt[:].rearrange("p (b q) t -> p b (q t)", b=BATCH)


def gate_chunk(pool, T, k):
    pool.wait_ge(T.y_moved, (k + 1) * (16 * Q * Q))
    part = by_channel(T)[:, :, bass.ds(k * CH, CH)]
    chunk_z = T.z[:, bass.ds(k % 2, 1), :].rearrange("p o (b t) -> p (o b) t", b=BATCH)
    return pool.tensor_tensor(part, part, chunk_z, ALU.mult)


def scan(nc, T):
    with ExitStack() as ctx:
        def sem(name):
            return ctx.enter_context(nc.semaphore("sc_" + name))

        def sb(name, shape, dt=F32):
            return ctx.enter_context(nc.sbuf_tensor("sc_" + name, shape, dt))

        conv_made, xc_made, xr_made, xq_made, c_product, c_made, b_product, b_taken, x_product, xd_made = map(
            sem, ("conv_made", "xc_made", "xr_made", "xq_made", "c_product", "c_made", "b_product", "b_taken", "x_product", "xd_made"))
        b_biased, wb_made, cb_made, u_made, y_made, y_taken = map(
            sem, ("b_biased", "wb_made", "cb_made", "u_made", "y_made", "y_taken"))
        z_made, z_taken = sem("z_made"), sem("z_taken")
        early_made, early_b_taken, early_x_taken, early_biased = map(
            sem, ("early_made", "early_b_taken", "early_x_taken", "early_biased"))
        y_turned, y_ordered = sem("y_turned"), sem("y_ordered")
        y_moved = T.y_moved
        steps = sem("steps")
        zeroed = sem("zeroed")

        TT = CH // Q
        warm = sb("warm", [P, 1])
        xc = sb("xc", [P, BATCH, CH])
        xr = sb("xr", [P, CH, Q, BATCH])
        xq = sb("xq", [P, CH, Q, BATCH])
        cr = sb("cr", [P, 2 * CH * BATCH])
        bq = sb("bq", [P, 2 * TT * ST])
        xd = T.share
        wb = [sb(f"wb{h}", [P, Q, P]) for h in range(2)]
        cb = [sb(f"cb{h}", [P, Q, GRP, P]) for h in range(2)]
        state = sb("state", [P, 2 * Q, GRP, HALF])
        scaled = sb("scaled", [P, GRP, HALF])
        BODIES = CH // (2 * Q)
        ys = sb("ys", [P, GRP, BODIES * ST])
        yt = T.yt
        ordered = lambda k: T.xa[:, :, bass.ds(k * CH, CH)].rearrange("p (h q) t -> p h q t", q=Q)
        z = T.z
        tokens = by_channel(T)
        y_all = tokens
        u_bank, y_bank, prep = T.bank[0:4], T.bank[4:6], T.bank[6:8]

        with nc.Block() as block:
            @block.tensor
            def _(pe):
                def project_z(k, more):
                    if more:
                        pe.wait_ge(b_taken, k + 2)
                    else:
                        pe.wait_ge(z_taken, k)
                    pe.matmul(prep[0][:], T.in_t[:, D:2 * D], tokens[:, :, bass.ds(k * CH, CH)],
                              start=True, stop=True).then_inc(z_made, 1)

                def convolve(k, tap):
                    made = pe.matmul(prep[0][:], T.conv_diag[:, tap, :], T.xa[:, :, bass.ds(k * CH + tap, CH)],
                                     start=(tap == 0), stop=(tap == 3))
                    if tap == 3:
                        made.then_inc(conv_made, 1)

                def project_c(k, bank):
                    pe.wait_ge(xc_made, k + 1)
                    if not (isinstance(k, int) and k == 0):
                        pe.wait_ge(xd_made, k)
                    pe.matmul(bank[:], T.c_rep[:].rearrange("p q n -> p (q n)"),
                              xc[:].rearrange("p b t -> p t b"), start=True, stop=True).then_inc(c_product, 1)

                def project_b(k, half, bank):
                    pe.wait_ge(xr_made, k + 1)
                    for tt in range(half * TT // 2, (half + 1) * TT // 2):
                        made = pe.matmul(bank[:, tt * ST:(tt + 1) * ST],
                                         xr[:, Q * tt:Q * tt + Q, :, :].rearrange("p t q b -> p (t q b)"), T.b_t[:],
                                         start=True, stop=True)
                    made.then_inc(b_product if half == 1 else early_made, 1)

                def regroup(k, tts, bank):
                    pe.wait_ge(xq_made, k + 1)
                    if not (isinstance(k, int) and k == 0):
                        pe.wait_ge(c_made, k + 1)
                    for tt in tts:
                        made = pe.matmul(bank[:, tt * ST:(tt + 1) * ST],
                                         xq[:, Q * tt:Q * tt + Q, :, :].rearrange("p t q b -> p (t q b)"), T.stack[:],
                                         start=True, stop=True)
                    made.then_inc(x_product if tts[-1] == TT - 1 else early_made, 1)

                def outer(q, h):
                    pe.wait_ge(wb_made, q + 1)
                    for m in range(2):
                        if not (isinstance(q, int) and q < 2):
                            pe.wait_ge(steps, (q * 2 + m - 4) * 12 + 10)
                        for i in range(2):
                            last = pe.matmul(u_bank[2 * h + m][:, i * 256:(i + 1) * 256], wb[h][:, 2 * m + i, :],
                                             xd[:, bass.ds(q % (2 * TT) * 256, 256)], start=True, stop=True)
                        last.then_inc(u_made, 1)

                def contract(q, h, n, bank):
                    pe.wait_ge(cb_made, q + 1)
                    if h == 0 and not (isinstance(q, int) and q < 4):
                        pe.wait_ge(y_taken, n - 1)
                    pe.wait_ge(steps, (q + 1) * 24)
                    for half in range(GRP):
                        for i in range(Q):
                            last = pe.matmul(bank[:, half * HALF:(half + 1) * HALF], cb[h][:, i, half, :], state[:, Q * h + i, half, :],
                                             start=(h == 0 and half == 0 and i == 0),
                                             stop=(h == 1 and half == GRP - 1 and i == Q - 1))
                    last.then_inc(y_made, 1)

                def chunk(k, more=True):
                    first = isinstance(k, int) and k == 0
                    late = 1 if first else 0
                    for j in range(TT):
                        q, h = k * TT + j, j % 2
                        piece = j - late
                        if j == TT - 1 and more:
                            pe.wait_ge(xd_made, k + 2)
                        if j == TT // 2 - 1 and first:
                            pe.wait_ge(xd_made, 1)
                        if j < TT - 1 or more:
                            outer(q + 1, 1 - h)
                        if j > 0 or not first:
                            contract(q - 1, 1 - h, k * BODIES + (j - 1) // 2, y_bank[(j - 1) // 2 % 2])
                        if j == 0 and first:
                            regroup(0, range(TT // 2, TT), prep[1])
                        if piece == 0 and more:
                            if first:
                                pe.wait_ge(b_taken, 1)
                            else:
                                pe.wait_ge(z_taken, k)
                        if 0 <= piece < 4 and more:
                            convolve(k + 1, piece)
                        if piece == 5 and more:
                            project_c(k + 1, prep[1])
                        if piece in (6, 8) and more:
                            project_b(k + 1, (piece - 6) // 2, prep[0])
                        if piece in (10, 12) and more:
                            regroup(k + 1, range((piece - 10) * TT // 4, (piece - 8) * TT // 4), prep[1])
                        if piece == 14:
                            project_z(k, more)

                for tap in range(4):
                    convolve(0, tap)
                project_b(0, 0, prep[0])
                regroup(0, range(0, TT // 4), prep[1])
                regroup(0, range(TT // 4, TT // 2), y_bank[1])
                project_c(0, u_bank[2])
                pe.wait_ge(early_x_taken, 2)
                outer(0, 0)
                project_b(0, 1, prep[0])
                pe.wait_ge(c_made, 1)
                chunk(0)
                with pe.Fori(1, NCH - 1) as k:
                    chunk(k)
                chunk(NCH - 1, more=False)
                contract(QUADS - 1, 1, L // 8 - 1, y_bank[1])

            @block.scalar
            def _(act):
                def take_conv(k):
                    act.wait_ge(conv_made, k + 1)
                    act.activation(xc[:].rearrange("p b t -> p (b t)"), prep[0][:], ACT.Silu, bias=T.cols[:, 2:3]).then_inc(xc_made, 1)
                    act.wait_ge(xc_made, k + 1)
                    if not (isinstance(k, int) and k == 0):
                        act.activation(xr[:], spread(xc[:, 0, 0:1], [[1, CH], [0, Q], [CH, BATCH]]), ACT.Copy).then_inc(xr_made, 1)
                    for dq in range(Q):
                        last = act.activation(xq[:, :, dq, :], xc[:].rearrange("p b t -> p t b"), ACT.Copy,
                                              scale=T.mask4[:, dq:dq + 1])
                    last.then_inc(xq_made, 1)

                def take_c(k, bank):
                    act.wait_ge(c_product, k + 1)
                    act.activation(cr[:, bass.ds(k % 2 * (CH * BATCH), CH * BATCH)], bank[:], ACT.Identity,
                                   bias=T.cols[:, 3:4]).then_inc(c_made, 1)

                def take_early_b():
                    act.wait_ge(early_made, 1)
                    act.activation(bq[:, 0:TT // 2 * ST], prep[0][:, 0:TT // 2 * ST], ACT.Copy).then_inc(early_b_taken, 1)

                def take_b(k):
                    act.wait_ge(b_product, k + 1)
                    act.activation(bq[:, bass.ds(k % 2 * (TT * ST), TT * ST)], prep[0][:], ACT.Copy).then_inc(b_taken, 1)

                def spread_x(k, tts, bank):
                    part = xd[:, bass.ds((k % 2 * TT + tts[0]) * 256, len(tts) * 256)].rearrange("p (t b g) -> p t b g", b=BATCH, g=ST)
                    for b in range(BATCH):
                        made = act.activation(part[:, :, b, :], bank[:, tts[0] * ST:(tts[-1] + 1) * ST].rearrange("p (t g) -> p t g", g=ST),
                                              ACT.Copy, scale=T.mask8[:, b:b + 1])
                    return made

                def take_x(k):
                    act.wait_ge(x_product, k + 1)
                    spread_x(k, range(TT), prep[1]).then_inc(xd_made, 1)

                def take_y(k, r):
                    act.wait_ge(y_made, (k * BODIES + r) * 2 + 2)
                    for b in range(Q):
                        rows = slice(ST * b, ST * b + ST)
                        for half in range(GRP):
                            at = half * HALF + ST * b
                            last = act.activation(ys[rows, half, r * ST:(r + 1) * ST], y_bank[r % 2][rows, at:at + ST], ACT.Copy)
                    last.then_inc(y_taken, 1)

                def order_y(k):
                    act.wait_ge(y_turned, k + 1)
                    if not (isinstance(k, int) and k == 0):
                        act.wait_ge(y_moved, k * (16 * Q * Q))
                    act.activation(ordered(k), yt[:].rearrange("p h (t q) -> p h q t", q=Q), ACT.Copy).then_inc(y_ordered, 1)

                def take_z(k):
                    act.wait_ge(z_made, k + 1)
                    act.activation(z[:, bass.ds(k % 2, 1), :].rearrange("p o w -> p (o w)"), prep[0][:], ACT.Silu,
                                   bias=T.cols[:, 1:2]).then_inc(z_taken, 1)

                def chunk(k, more=True):
                    first = isinstance(k, int) and k == 0
                    if not first:
                        act.wait_ge(y_turned, k)
                    take_y(k, 0)
                    if first:
                        take_y(k, 1)
                    if more:
                        take_conv(k + 1)
                    if not first:
                        take_y(k, 1)
                    if more:
                        take_c(k + 1, prep[1])
                    take_y(k, 2)
                    if not first:
                        order_y(k - 1)
                    take_y(k, 3)
                    if more:
                        take_b(k + 1)
                    take_y(k, 4)
                    take_y(k, 5)
                    if more:
                        take_x(k + 1)
                    take_y(k, 6)
                    take_z(k)
                    take_y(k, 7)

                act.activation(warm[:], T.mask4[:, 0:1], ACT.Silu)
                take_conv(0)
                take_early_b()
                act.wait_ge(early_made, 3)
                spread_x(0, range(TT // 4, TT // 2), y_bank[1]).then_inc(early_x_taken, 1)
                take_c(0, u_bank[2])
                act.wait_ge(b_product, 1)
                act.activation(bq[:, TT // 2 * ST:TT * ST], prep[0][:, TT // 2 * ST:], ACT.Copy).then_inc(b_taken, 1)
                act.wait_ge(x_product, 1)
                spread_x(0, range(TT // 2, TT), prep[1]).then_inc(xd_made, 1)
                chunk(0)
                with act.Fori(1, NCH - 1) as k:
                    chunk(k)
                chunk(NCH - 1, more=False)

            @block.sync
            def _(sp):
                def move_y(k):
                    sp.wait_ge(y_ordered, k + 1)
                    for b in range(Q):
                        for dq in range(Q):
                            to = y_all[ST * dq:ST * dq + ST, b::Q, bass.ds(k * CH, CH)]
                            sp.dma_start(to, ordered(k)[ST * b:ST * b + ST, :, dq, :]).then_inc(y_moved, 16)

                with sp.Fori(0, NCH - 1) as k:
                    move_y(k)

            @block.gpsimd
            def _(pool):
                pool.memset(state[:, 2 * Q - 1, :, :], 0.0).then_inc(zeroed, 1)
                for h in range(2):
                    pool.memset(cb[h][:], 0.0).then_inc(zeroed, 1)
                pool.wait_ge(zeroed, 3)
                pool.wait_ge(T.small_in, 16 * (7 + Q))

                def add_bias(k):
                    if not (isinstance(k, int) and k == 0):
                        pool.wait_ge(c_made, k + 1)
                    pool.wait_ge(b_taken, k + 1)
                    part = bq[:, bass.ds(k % 2 * (TT * ST), TT * ST)].rearrange("p (t n) -> p t n", n=ST)
                    pool.tensor_tensor(part, part, spread(T.bb_row[:], [[0, TT], [1, ST]]), ALU.add).then_inc(b_biased, 1)
                    pool.wait_ge(b_biased, k + 1)

                def expand_b(q, h):
                    if not (isinstance(q, int) and q < 2):
                        pool.wait_ge(u_made, (q - 1) * 2)
                    b_row = bq[:, bass.ds(q % (2 * TT) * ST, ST)]
                    pool.tensor_tensor(wb[h][:].rearrange("p t (q n) -> p (t q) n", n=ST), repeat_outer(b_row, Q * Q),
                                       spread(T.mask16[:], [[1, Q * Q], [0, ST]]), ALU.mult).then_inc(wb_made, 1)

                def expand_c(q, h):
                    if not (isinstance(q, int) and q < 2):
                        pool.wait_ge(y_made, q - 1)
                    c_row = cr[:, bass.ds(q % (2 * TT) * (Q * BATCH), Q * BATCH)]
                    at = Q * Q * h
                    pool.tensor_tensor(spread(cb[h][:, 0, 0, at:at + 1], [[GRP * P + Q, Q], [ST, BATCH], [1, Q]]),
                                       c_row.rearrange("p (t b) -> p t b", b=BATCH).unsqueeze(3).to_broadcast([P, Q, BATCH, Q]),
                                       spread(T.mask4[:], [[0, Q], [0, BATCH], [1, Q]]), ALU.mult).then_inc(cb_made, 1)

                def two_quads(n):
                    for h in range(2):
                        expand_b(n * 2 + h + 2, h)
                        expand_c(n * 2 + h, h)

                def gate(k):
                    pool.wait_ge(z_taken, k + 1)
                    gate_chunk(pool, T, k)

                def bias(k):
                    for t, row in ((T.xn, 0), (T.x, 2)):
                        part = t[:, bass.ds(k * (NT // NCH), NT // NCH), :]
                        pool.tensor_tensor(part, part, spread(T.rows[:, row, :], [[0, NT // NCH], [1, D]]), ALU.add)

                bias(0)
                halves = [bq[:, h * TT // 2 * ST:(h + 1) * TT // 2 * ST].rearrange("p (t n) -> p t n", n=ST) for h in range(2)]
                pool.wait_ge(early_b_taken, 1)
                pool.tensor_tensor(halves[0], halves[0], spread(T.bb_row[:], [[0, TT // 2], [1, ST]]), ALU.add).then_inc(early_biased, 1)
                pool.wait_ge(early_biased, 1)
                expand_b(0, 0)
                expand_b(1, 1)
                pool.wait_ge(c_made, 1)
                two_quads(0)
                pool.wait_ge(b_taken, 1)
                pool.tensor_tensor(halves[1], halves[1], spread(T.bb_row[:], [[0, TT // 2], [1, ST]]), ALU.add).then_inc(b_biased, 1)
                pool.wait_ge(b_biased, 1)
                with pool.Fori(1, 7) as n:
                    two_quads(n)
                add_bias(1)
                two_quads(7)
                with pool.Fori(1, NCH - 1) as k:
                    with pool.Fori(0, 7) as n:
                        two_quads(k * 8 + n)
                    add_bias(k + 1)
                    two_quads(k * 8 + 7)
                    gate(k - 1)
                    bias(k)
                bias(NCH - 1)
                with pool.Fori((NCH - 1) * 8, NCH * 8 - 1) as n:
                    two_quads(n)
                for h in range(2):
                    expand_c(QUADS - 2 + h, h)

            @block.vector
            def _(dve):
                decay = spread(T.decay[:], [[0, Q], [1, ST]])
                by_b = lambda t: t.rearrange("p (b g) -> p b g", g=ST)

                def eight_steps(n):
                    for r in range(2 * Q):
                        t = n * 8 + r
                        start = isinstance(n, int) and t == 0
                        old, new = (r - 1) % (2 * Q), r
                        for half in range(GRP):
                            if start:
                                dve.wait_ge(zeroed, 1)
                            else:
                                dve.wait_ge(steps, t * 6 - 1 + half)
                            dve.tensor_tensor(by_b(scaled[:, half, :]), by_b(state[:, old, half, :]), decay,
                                              ALU.mult).then_inc(steps, 1)
                        if r % 2 == 0:
                            dve.wait_ge(u_made, n * 4 + r // 2 + 1)
                        for half in range(GRP):
                            dve.wait_ge(steps, t * 6 + 1 + half)
                            at = r % 2 * 256 + half * HALF
                            dve.tensor_tensor(scaled[:, half, :], scaled[:, half, :], u_bank[r // 2][:, at:at + HALF],
                                              ALU.add).then_inc(steps, 1)
                        if r % Q == 0 and not (isinstance(n, int) and n == 0):
                            dve.wait_ge(y_made, n * 2 + r // Q - 1)
                        for half in range(GRP):
                            dve.wait_ge(steps, t * 6 + 3 + half)
                            dve.tensor_scalar(state[:, new, half, :], scaled[:, half, :], 10.0, -10.0, ALU.min, ALU.max).then_inc(steps, 1)

                def turn_y(k):
                    dve.wait_ge(y_taken, (k + 1) * 8)
                    for half in range(GRP):
                        last = dve.transpose(yt[:, half, :], ys[:, half, :])
                    last.then_inc(y_turned, 1)

                dve.wait_ge(xc_made, 1)
                dve.tensor_copy(xr[:], spread(xc[:, 0, 0:1], [[1, CH], [0, Q], [CH, BATCH]])).then_inc(xr_made, 1)
                dve.wait_ge(early_made, 2)
                part = xd[:, 0:TT // 4 * 256].rearrange("p (t b g) -> p t b g", b=BATCH, g=ST)
                for b in range(BATCH):
                    last = dve.tensor_scalar(part[:, :, b, :], prep[1][:, 0:TT // 4 * ST].rearrange("p (t g) -> p t g", g=ST),
                                             T.mask8[:, b:b + 1], None, ALU.mult)
                last.then_inc(early_x_taken, 1)

                for n in range(BODIES):
                    eight_steps(n)
                with dve.Fori(1, NCH) as k:
                    eight_steps(k * BODIES)
                    turn_y(k - 1)
                    for r in range(1, BODIES):
                        eight_steps(k * BODIES + r)
                turn_y(NCH - 1)


def repeat_outer(ap, n):
    return ap.unsqueeze(1).to_broadcast([ap.shape[0], n, ap.shape[1]])


def finish_attention(nc, T):
    with ExitStack() as ctx:
        def sem(name):
            return ctx.enter_context(nc.semaphore("fa_" + name))

        made, h_added, x_scaled, x_made, gated, moved, last_gated = map(
            sem, ("made", "h_added", "x_scaled", "x_made", "gated", "moved", "last_gated"))
        H = Normalization(ctx, nc, T, "nh_", T.xn, TIME_GROUPS)
        N = Normalization(ctx, nc, T, "n1_", T.x, TIME_GROUPS)
        sums = [T.bank[0:2], T.bank[2:4]]
        banks = T.bank[4:6]
        with nc.Block() as block:
            @block.vector
            def _(dve):
                for g in range(GROUPS + 2):
                    if g < GROUPS:
                        dve.wait_ge(made, g + 1)
                        for half in range(2):
                            tiles = H.tiles[g][4 * half:4 * half + 4]
                            part = T.xn[:, tiles[0]:tiles[3] + 1:tiles[1] - tiles[0], :]
                            dve.tensor_tensor(part, sums[g % 2][half][:].rearrange("p (j d) -> p j d", d=D), part,
                                              ALU.add).then_inc(h_added, 1)
                        dve.wait_ge(h_added, 2 * g + 2)
                        H.take_stats(dve, g)
                        H.aggregate(dve, g)
                    if g == 0:
                        for b in range(Q):
                            dve.wait_ge(moved, b + 1)
                            dve.tensor_tensor(by_channel(T)[:, b::Q, (NCH - 1) * CH:],
                                              T.bank[4 + b][:, 0:GRP * CH].rearrange("p (h t) -> p h t", h=GRP),
                                              T.z[:, (NCH - 1) % 2, :].rearrange("p (b t) -> p b t", b=BATCH)[:, b::Q, :],
                                              ALU.mult).then_inc(last_gated, 1)
                    if g >= 2:
                        dve.wait_ge(x_made, g - 1)
                        N.take_stats(dve, g - 2)
                        N.aggregate(dve, g - 2)
                    if g < GROUPS:
                        H.invert(dve, g)
                    if g >= 2:
                        N.invert(dve, g - 2)
                        N.normalize_dve(dve, g - 2)

            @block.scalar
            def _(act):
                for g in range(GROUPS + 2):
                    if g < GROUPS:
                        H.take_root(act, g)
                    if g >= 2:
                        N.take_root(act, g - 2)
                    if g < GROUPS:
                        H.normalize_act(act, g, share=range(GT))
                    if g >= 2:
                        N.normalize_act(act, g - 2)
                        N.take_transposed(act, g - 2, banks)

            @block.gpsimd
            def _(pool):
                gate_chunk(pool, T, NCH - 2).then_inc(gated, 1)
                for g, group in enumerate(TIME_GROUPS):
                    pool.wait_ge(H.act_normed, (g + 1) * GT)
                    pool.tensor_tensor(T.xn[:, group, :], T.xn[:, group, :], spread(T.rows[:, 1, :], [[0, GT], [1, D]]),
                                       ALU.mult).then_inc(x_scaled, 1)
                    pool.wait_ge(x_scaled, g + 1)
                    pool.tensor_tensor(T.x[:, group, :], T.x[:, group, :], T.xn[:, group, :], ALU.add).then_inc(x_made, 1)

            @block.tensor
            def _(pe):
                def project(g):
                    if g == GROUPS - 1:
                        pe.wait_ge(gated, 1)
                        pe.wait_ge(last_gated, Q)
                    if g >= 2:
                        pe.wait_ge(h_added, 2 * g - 2)
                    for n, j in enumerate(H.tiles[g]):
                        last = pe.matmul(sums[g % 2][n // 4][:, n % 4 * D:(n % 4 + 1) * D], T.xt[:, j, :], T.o_t[:],
                                         start=True, stop=True)
                    last.then_inc(made, 1)

                project(0)
                for b in range(Q):
                    rows = slice(ST * b, ST * b + ST)
                    for half in range(GRP):
                        for dq in range(Q):
                            last = pe.matmul(T.bank[4 + b][ST * dq:ST * dq + ST, half * CH:(half + 1) * CH],
                                             T.ident[rows, rows], T.yt[rows, half, dq::Q], start=True, stop=True)
                    last.then_inc(moved, 1)
                for g in range(1, GROUPS):
                    project(g)
                pe.wait_ge(last_gated, Q)
                for g in range(GROUPS):
                    N.transpose(pe, g, banks)
                    N.logits(pe, g)

            @block.sync
            def _(sp):
                N.store_tokens(sp, 1)


_INS = ["L0_attn_x", "L0_attn_in_w", "L0_attn_in_b", "L0_attn_conv_w", "L0_attn_conv_b", "L0_attn_A_log", "L0_attn_B_w",
        "L0_attn_B_b", "L0_attn_C_w", "L0_attn_C_b", "L0_attn_out_w", "L0_attn_out_b", "L0_attn_ln_w", "L0_attn_ln_b",
        "L0_ffn_Wr", "L0_ffn_W1", "L0_ffn_b1", "L0_ffn_W2", "L0_ffn_b2"]


def kernel(**inputs):
    import numpy as np
    import concourse.bacc as bacc
    from concourse.bass_utils import run_bass_kernel_spmd

    nc = bacc.Bacc("TRN2", target_bir_lowering=False, num_devices=1)
    arrays, args = {}, {}
    for name in _INS:
        array = np.ascontiguousarray(inputs[name])
        arrays[name] = array
        args[name] = nc.dram_tensor(name, array.shape, mybir.dt.from_np(array.dtype), kind="ExternalInput").ap()
    out = nc.dram_tensor("out", (BATCH, L, D), F32, kind="ExternalOutput").ap()
    build(nc, args, out)
    results = run_bass_kernel_spmd(nc, [arrays], core_ids=[0])
    return results.results[0]["out"]
```
